# Optimizing a Trainium2 kernel written in Bass

```python
import numpy as np
import jax
import jax.numpy as jnp

def _softmax(x, axis=-1):
    return jax.nn.softmax(x, axis=axis)
def _gelu(x):
    return jax.nn.gelu(x, approximate=True)
def _silu(x):
    return jax.nn.silu(x)
def _sigmoid(x):
    return jax.nn.sigmoid(x)
def _layernorm(x, axis=-1, eps=1e-5):
    m = jnp.mean(x, axis=axis, keepdims=True)
    v = jnp.var(x, axis=axis, keepdims=True)
    return (x - m) / jnp.sqrt(v + eps)
def _scatter_add(tgt, idx, src, axis=0):
    return tgt.at[idx].add(src)
def _segment_sum(src, seg, n):
    return jax.ops.segment_sum(src, seg, n)

kernel_name = 'mk_conv_seq_d2_conv_nchw512_80eca2'

def setup_inputs(seed: int = 0):
    np.random.seed(seed)
    _w = jnp.asarray
    def _rec_inputs():
        import jax
        import jax.numpy as jnp
        _gk = jax.random.key(seed)
        x = -0.0002928 + 1 * jax.random.normal(jax.random.fold_in(_gk, 1), (8, 512, 32, 32), jnp.float32)
        return x
    x = _rec_inputs()
    def _L0_conv_setup():
        import jax, jax.numpy as jnp
        import numpy as np
        B, C, H, W = (8, 512, 32, 32)
        HEADS = 8
        EPS = 1e-05

        def conv1x1(X, Wt, b):
            return jnp.einsum('co,bohw->bchw', Wt, X) + b[None, :, None, None]
        key = jax.random.key(seed)
        ks = jax.random.split(key, 9)
        s = 0.02
        f32 = jnp.float32
        return {'X': jax.random.normal(ks[0], (B, C, H, W), f32), 'Wq': jax.random.normal(ks[1], (C, C), f32) * s, 'bq': jnp.zeros((C,), f32), 'Wk': jax.random.normal(ks[2], (C, C), f32) * s, 'bk': jnp.zeros((C,), f32), 'Wv': jax.random.normal(ks[3], (C, C), f32) * s, 'bv': jnp.zeros((C,), f32), 'Wo': jax.random.normal(ks[4], (C, C), f32) * s, 'bo': jnp.zeros((C,), f32), 'gamma': jnp.ones((C,), f32), 'beta': jnp.zeros((C,), f32)}
    _L0_conv_all = _L0_conv_setup()
    _L0_conv_in = {k: v for k, v in _L0_conv_all.items() if k in ('Wq', 'bq', 'Wk', 'bk', 'Wv', 'bv', 'Wo', 'bo', 'gamma', 'beta', )}
    del _L0_conv_all

    def _L1_conv_setup():
        import jax, jax.numpy as jnp
        import numpy as np
        B, C, H, W = (8, 512, 32, 32)
        NUM_HEADS = 8
        NUM_GROUPS = 32
        EPS = 1e-05

        def _group_norm(x, gamma, beta):
            b, c, l = x.shape
            xg = x.reshape(b, NUM_GROUPS, c // NUM_GROUPS * l)
            mean = jnp.mean(xg, axis=-1, keepdims=True)
            var = jnp.var(xg, axis=-1, keepdims=True)
            xn = ((xg - mean) * jax.lax.rsqrt(var + EPS)).reshape(b, c, l)
            return xn * gamma[None, :, None] + beta[None, :, None]
        key = jax.random.key(seed)
        ks = jax.random.split(key, 7)
        x = jax.random.normal(ks[0], (B, C, H, W), dtype=jnp.float32)
        gamma = jnp.ones((C,), dtype=jnp.float32)
        beta = jnp.zeros((C,), dtype=jnp.float32)
        w_qkv = jax.random.normal(ks[1], (3 * C, C), dtype=jnp.float32) * (1.0 / np.sqrt(C))
        b_qkv = jax.random.normal(ks[2], (3 * C,), dtype=jnp.float32) * 0.01
        w_proj = jax.random.normal(ks[3], (C, C), dtype=jnp.float32) * (1.0 / np.sqrt(C))
        b_proj = jax.random.normal(ks[4], (C,), dtype=jnp.float32) * 0.01
        return {'x': x, 'gamma': gamma, 'beta': beta, 'w_qkv': w_qkv, 'b_qkv': b_qkv, 'w_proj': w_proj, 'b_proj': b_proj}
    _L1_conv_all = _L1_conv_setup()
    _L1_conv_in = {k: v for k, v in _L1_conv_all.items() if k in ('gamma', 'beta', 'w_qkv', 'b_qkv', 'w_proj', 'b_proj', )}
    del _L1_conv_all

    return {
        "x": x,
        "L0_conv_Wq": _L0_conv_in["Wq"],
        "L0_conv_bq": _L0_conv_in["bq"],
        "L0_conv_Wk": _L0_conv_in["Wk"],
        "L0_conv_bk": _L0_conv_in["bk"],
        "L0_conv_Wv": _L0_conv_in["Wv"],
        "L0_conv_bv": _L0_conv_in["bv"],
        "L0_conv_Wo": _L0_conv_in["Wo"],
        "L0_conv_bo": _L0_conv_in["bo"],
        "L0_conv_gamma": _L0_conv_in["gamma"],
        "L0_conv_beta": _L0_conv_in["beta"],
        "L1_conv_gamma": _L1_conv_in["gamma"],
        "L1_conv_beta": _L1_conv_in["beta"],
        "L1_conv_w_qkv": _L1_conv_in["w_qkv"],
        "L1_conv_b_qkv": _L1_conv_in["b_qkv"],
        "L1_conv_w_proj": _L1_conv_in["w_proj"],
        "L1_conv_b_proj": _L1_conv_in["b_proj"],
    }

def reference(x, L0_conv_Wq, L0_conv_bq, L0_conv_Wk, L0_conv_bk, L0_conv_Wv, L0_conv_bv, L0_conv_Wo, L0_conv_bo, L0_conv_gamma, L0_conv_beta, L1_conv_gamma, L1_conv_beta, L1_conv_w_qkv, L1_conv_b_qkv, L1_conv_w_proj, L1_conv_b_proj):
    import jax
    import jax.numpy as jnp
    def _L0_conv_ref(X, Wq, bq, Wk, bk, Wv, bv, Wo, bo, gamma, beta):
        import jax, jax.numpy as jnp
        import numpy as np
        B, C, H, W = (8, 512, 32, 32)
        HEADS = 8
        EPS = 1e-05

        def conv1x1(X, Wt, b):
            return jnp.einsum('co,bohw->bchw', Wt, X) + b[None, :, None, None]
        b, c, h, w = X.shape
        d = c // HEADS
        n = h * w
        K = conv1x1(X, Wq, bq).reshape(b, HEADS, d, n)
        Q = conv1x1(X, Wk, bk).reshape(b, HEADS, d, n)
        V = conv1x1(X, Wv, bv).reshape(b, HEADS, d, n)
        M = jnp.einsum('bhmn,bhen->bhme', K, V)
        Out = jnp.einsum('bhme,bhmn->bhen', M, Q)
        Out = Out.reshape(b, c, h, w)
        Out = conv1x1(Out, Wo, bo) + X
        mean = Out.mean(axis=(0, 2, 3), keepdims=True)
        var = Out.var(axis=(0, 2, 3), keepdims=True)
        Out = (Out - mean) * jax.lax.rsqrt(var + EPS)
        return Out * gamma[None, :, None, None] + beta[None, :, None, None]

    def _L1_conv_ref(x, gamma, beta, w_qkv, b_qkv, w_proj, b_proj):
        import jax, jax.numpy as jnp
        import numpy as np
        B, C, H, W = (8, 512, 32, 32)
        NUM_HEADS = 8
        NUM_GROUPS = 32
        EPS = 1e-05

        def _group_norm(x, gamma, beta):
            b, c, l = x.shape
            xg = x.reshape(b, NUM_GROUPS, c // NUM_GROUPS * l)
            mean = jnp.mean(xg, axis=-1, keepdims=True)
            var = jnp.var(xg, axis=-1, keepdims=True)
            xn = ((xg - mean) * jax.lax.rsqrt(var + EPS)).reshape(b, c, l)
            return xn * gamma[None, :, None] + beta[None, :, None]
        b, c, h, w = x.shape
        L = h * w
        xf = x.reshape(b, c, L)
        xn = _group_norm(xf, gamma, beta)
        qkv = jnp.einsum('oc,bcl->bol', w_qkv, xn) + b_qkv[None, :, None]
        ch = c // NUM_HEADS
        q, k, v = jnp.split(qkv, 3, axis=1)
        bh = b * NUM_HEADS
        q = q.reshape(bh, ch, L)
        k = k.reshape(bh, ch, L)
        v = v.reshape(bh, ch, L)
        scale = 1.0 / np.sqrt(np.sqrt(ch))
        weight = jnp.einsum('bct,bcs->bts', q * scale, k * scale)
        weight = jax.nn.softmax(weight.astype(jnp.float32), axis=-1).astype(q.dtype)
        a = jnp.einsum('bts,bcs->bct', weight, v)
        hid = a.reshape(b, c, L)
        hid = jnp.einsum('oc,bcl->bol', w_proj, hid) + b_proj[None, :, None]
        return (xf + hid).reshape(b, c, h, w)

    def _gn(v, G=32, eps=1e-5):
        B_, C_, H_, W_ = v.shape
        g = v.reshape(B_, G, C_ // G, H_, W_)
        m = jnp.mean(g, axis=(2, 3, 4), keepdims=True)
        s = jnp.var(g, axis=(2, 3, 4), keepdims=True)
        return ((g - m) / jnp.sqrt(s + eps)).reshape(v.shape)

    def _ln_c(v, eps=1e-6):
        m = jnp.mean(v, axis=1, keepdims=True)
        s = jnp.var(v, axis=1, keepdims=True)
        return (v - m) / jnp.sqrt(s + eps)

    def _ln_t(v, eps=1e-5):
        m = jnp.mean(v, axis=-1, keepdims=True)
        s = jnp.var(v, axis=-1, keepdims=True)
        return (v - m) / jnp.sqrt(s + eps)

    def _to_tokens(v):
        B_, C_, H_, W_ = v.shape
        return v.reshape(B_, C_, H_ * W_).transpose(0, 2, 1)
    def _from_tokens(t, like):
        B_, C_, H_, W_ = like.shape
        return t.transpose(0, 2, 1).reshape(B_, C_, H_, W_)

    x = _L0_conv_ref(x, L0_conv_Wq, L0_conv_bq, L0_conv_Wk, L0_conv_bk, L0_conv_Wv, L0_conv_bv, L0_conv_Wo, L0_conv_bo, L0_conv_gamma, L0_conv_beta)
    x = _L1_conv_ref(x, L1_conv_gamma, L1_conv_beta, L1_conv_w_qkv, L1_conv_b_qkv, L1_conv_w_proj, L1_conv_b_proj)
    return x


_drawn_inputs = setup_inputs


def setup_inputs(seed=0):
    import zlib

    import numpy as np

    out = dict(_drawn_inputs(seed))
    spreads = {'L0_conv_bq': (0.0, 0.1),
     'L0_conv_bk': (0.0, 0.1),
     'L0_conv_bv': (0.0, 0.1),
     'L0_conv_bo': (0.0, 0.8),
     'L0_conv_gamma': (1.0, 0.2),
     'L0_conv_beta': (0.0, 0.1),
     'L1_conv_gamma': (1.0, 0.2),
     'L1_conv_beta': (0.0, 0.1)}
    factors = {'L1_conv_b_qkv': 6.138, 'L1_conv_b_proj': 6.26}
    for name, (base, spread) in spreads.items():
        noise = np.random.default_rng([zlib.crc32(name.encode()), seed]).standard_normal(out[name].shape)
        drawn = base * np.exp(spread * noise) if base else spread * noise
        out[name] = jnp.asarray(drawn.astype(out[name].dtype))
    for name, factor in factors.items():
        out[name] = (out[name] * factor).astype(out[name].dtype)
    return out
```

```python
from contextlib import ExitStack

import numpy as np

import concourse.bass as bass
from concourse import mybir

F32 = mybir.dt.float32
F32R = mybir.dt.float32r
BF16 = mybir.dt.bfloat16
ALU = mybir.AluOpType
ACT = mybir.ActivationFunctionType
AX_X = mybir.AxisListType.X

B, C, N = 8, 512, 1024
P = 128
HEADS = 8
D = C // HEADS
CT = C // P
NT = N // P
HALF = 512
NH = N // HALF
GROUPS = 32
GC = C // GROUPS
EPS = 1e-5
GRAN = 16
HI, LO = 0, 1
THREE = ((HI, HI), (HI, LO), (LO, HI))


class Arena:

    def __init__(self, tensor, size):
        self.tensor, self.size, self.at = tensor, size, 0

    def take(self, *shape):
        n = int(np.prod(shape))
        assert self.at + n <= self.size, (self.at, n, self.size)
        view = self.tensor[:, self.at:self.at + n]
        self.at += n
        if len(shape) > 1:
            names = "abcdef"[:len(shape)]
            view = view.rearrange(f"p ({' '.join(names)}) -> p {' '.join(names)}",
                                  **dict(zip(names[1:], shape[1:])))
        return view


def f(ap):
    return ap.bitcast(F32)


def build(nc, x, wq_t, wv_t, wk, wo_t, bq0, bv0, bk0, bo0, gamma0, beta0, gamma1, beta1, w1, bqkv1, bproj1, out):
    y_dram = nc.dram_tensor("y_dram", [B, C, N], F32).ap()
    w1_dram = nc.dram_tensor("w1_dram", [GRAN, P, 2, CT, P], F32R).ap()

    x_v = x.rearrange("b (j p) n -> b p j n", p=P)
    y_v = y_dram.rearrange("b (j p) n -> b p j n", p=P)
    out_v = out.rearrange("b (j p) n -> b p j n", p=P)

    def rows(w):
        return w.rearrange("(j p) m -> p j m", p=P)

    def column(v):
        return v.rearrange("(j p) -> p j", p=P)

    with ExitStack() as ctx:
        def sb(name, shape, dt):
            return ctx.enter_context(nc.sbuf_tensor(name, shape, dt))

        def sem(name):
            return ctx.enter_context(nc.semaphore(name))

        R_SIZE, A_SIZE = 152 * 256, 50 * 256
        r_all = sb("r_all", [P, R_SIZE], F32R)
        a_all = sb("a_all", [P, A_SIZE], F32)

        r0, a0 = Arena(r_all, R_SIZE), Arena(a_all, A_SIZE)
        w_q, w_v, w_k, w_o = (r0.take(2, CT, C) for _ in range(4))
        xs = r0.take(2, CT, N)
        ks, vs = r0.take(2, 2, C), r0.take(2, 2, C)
        us, a_s = r0.take(2, CT, C), r0.take(2, CT, C)
        ms = r0.take(2, CT, P)
        gran_s = r0.take(2, CT, P)
        x32 = a0.take(CT, N)
        y32 = a0.take(2, CT, HALF)
        kv32 = a0.take(2, C)
        bias_rows = a0.take(2, C)
        eye_wide = a0.take(C + C - P)
        gran32 = a0.take(CT, P)
        stats = a0.take(CT, B * NH, 6)
        group_avg = a0.take(P)
        w32 = y32.rearrange("p a j n -> p a (j n)").rearrange("p a (j m) -> p a j m", j=CT)

        r1, a1 = Arena(r_all, R_SIZE), Arena(a_all, A_SIZE)
        w_v1 = r1.take(CT, 2, CT, P)
        w_s = r1.take(2, 2, 2, CT, P)
        xn = r1.take(2, CT, N)
        q_a = r1.take(2, 2, N)
        k_a = r1.take(2, 2, N)
        k_b = r1.take(2, 2, N)
        q_b = r1.take(2, N)
        hid = r1.take(2, CT, N)
        v_t = a1.take(NT, C)
        probs = a1.take(2, 2, N)
        res32 = probs.rearrange("p a h n -> p (a h) n")
        y_half = a1.take(2, HALF)
        p_sum = a1.take(2, N)
        o32 = a1.take(N)
        recip = a1.take(HALF)

        SMALL = 720
        small = sb("small", [P, SMALL], F32)
        s = Arena(small, SMALL)
        eye = s.take(P)
        ones64 = s.take(D)
        max2 = s.take(2, NT, NH)
        max_cols = s.take(4, 32)
        mean_var = s.take(CT, B, 2)
        bn_mv = s.take(CT, 2)
        bn_var = s.take(CT)
        root_tmp = s.take(CT * B)
        gn_in = s.take(CT, B)
        gn_mean = s.take(CT, B)
        x1_mean = s.take(CT, B)
        gn_tmp = s.take(CT, B)
        xn_scale, xn_bias = s.take(CT, B), s.take(CT, B)
        bn_scale, bn_bias, res_bias = s.take(CT), s.take(CT), s.take(CT)
        c_sum, c_vec = s.take(CT), s.take(CT)
        bo_c, bk_c, g0_c, b0_c, g1_c, b1_c, bp_c = (s.take(CT) for _ in range(7))
        bqkv_c = s.take(3 * CT)
        bk_s = sb("bk_s", [P, CT, 2], F32R)
        mask = sb("mask", [64, NT, P], BF16)

        psum = [ctx.enter_context(nc.psum_tensor(f"psum{i}", [P, 2, HALF], F32)) for i in range(4)]

        def bank(i):
            return psum[i // 2][:, i % 2, :]

        w_loaded = [sem("w_loaded0"), sem("w_loaded1")]
        consts_loaded = sem("consts_loaded")
        x_loaded = [sem(f"x_loaded{h}") for h in range(NH)]
        y_stored = [sem(f"y_stored{h}") for h in range(NH)]
        w_hi_done = sem("w_hi_done")
        w_lo_done = sem("w_lo_done")
        consts_ready = sem("consts_ready")
        dve_step = sem("dve_step")
        pool_step = sem("pool_step")
        x_hi_done = sem("x_hi_done")
        x_lo_done = sem("x_lo_done")
        ring_full = sem("ring_full")
        ring_free = sem("ring_free")
        hi_done = sem("hi_done")
        lo_done = sem("lo_done")
        kv_used = sem("kv_used")
        m_full = sem("m_full")
        m_split = sem("m_split")
        c_full = sem("c_full")
        c_ready = sem("c_ready")
        y_full = sem("y_full")
        y_ready = sem("y_ready")
        y_counted = sem("y_counted")
        gran_loaded = sem("gran_loaded")
        gran_split = sem("gran_split")
        gran_stored = sem("gran_stored")
        pads_ready = sem("pads_ready")
        gn_moved = sem("gn_moved")
        gn_averaged = sem("gn_averaged")
        norm_ready = sem("norm_ready")
        var_ready = sem("var_ready")
        root_ready = sem("root_ready")
        wv1_loaded = sem("wv1_loaded")
        ws_loaded = [sem("ws_loaded0"), sem("ws_loaded1")]
        y_half_loaded = [sem("y_half_loaded0"), sem("y_half_loaded1")]
        xn_made = sem("xn_made")
        xn_hi_done = sem("xn_hi_done")
        xn_lo_done = sem("xn_lo_done")
        work_full = sem("work_full")
        work_free = sem("work_free")
        qk_hi_done = sem("qk_hi_done")
        k_twice = sem("k_twice")
        max_ready = sem("max_ready")
        q_b_ready = sem("q_b_ready")
        scores_full = sem("scores_full")
        probs_ready = sem("probs_ready")
        pv_done = sem("pv_done")
        sum_step = sem("sum_step")
        o_ready = sem("o_ready")
        o_normed = sem("o_normed")
        hid_hi_done = sem("hid_hi_done")
        hid_lo_done = sem("hid_lo_done")
        res_loaded = sem("res_loaded")
        res_scaled = sem("res_scaled")
        out_stored = [sem("out_stored0"), sem("out_stored1")]

        block = ctx.enter_context(nc.Block())

        KV, U0, A0, RING0 = 2 * NT, 2 * NT, 2 * NT + CT, 2 * NT + 2 * CT
        FREE0 = KV + CT

        def ring_bank(t):
            return bank(4 + t % 4)

        PAIRS = CT
        QK, SMAX, SUMS = 2 * NH, 2 * NT * NH, NH
        WORK0 = QK + SMAX + 1 + NT
        WORK = PAIRS * (QK + SMAX + 1 + SUMS) + NT + CT * NH
        assert WORK % 2 == 0
        NEXT = QK + SMAX + 1

        def qk_used(b, p):
            return b * WORK + (WORK0 + p * (NEXT + SUMS) + QK)

        def sums_used(b, p, last):
            if p == 0:
                return b * WORK + (WORK0 - CT * NH - (NT - 5))
            return b * WORK + (WORK0 + p * (NEXT + SUMS) + (0 if last and p == PAIRS - 1 else QK // 2))

        def proj_used(b, t, last):
            return b * WORK + (WORK0 + WORK - CT * NH - (NEXT + NT if last else 0) + t)

        ROWS = (0, 0, 3, 6, 6, 6, 6, 5)
        PLACE0 = (0, 0, 4, 0, 0, 0, 0, 0)
        assert len(ROWS) == NT and sum(ROWS) == SMAX
        NORM_ROW = (-1, -1, 4, 7, 11, 14, 18, 22)
        LO_ROW = (0, 1, 6, 9, 13, 16, 20, 24)

        SCALE = 1.0 / float(np.sqrt(D))

        ONE = 1

        class Tally:

            def __init__(self):
                self.base, self.n, self.started = 0, 0, False

            def start(self, b):
                self.base, self.n, self.started = b * WORK, WORK0, True

            def next(self):
                self.n += 1
                return self.base + self.n, bank(6 + self.n % 2)

            def upto(self, n=0):
                return self.base + self.n - n

        @block.sync
        def _(sp):
            weights = (wq_t, wv_t, wk, wo_t)
            for w in range(2):
                sp.dma_start(w32[:, w], rows(weights[w])).then_inc(w_loaded[w], 16)
            for h in range(NH):
                sp.dma_start(x32[:, :, h * HALF:(h + 1) * HALF], x_v[0, :, :, h * HALF:(h + 1) * HALF]).then_inc(x_loaded[h], 16)
            for i, (to, of) in enumerate((
                    (bias_rows[:, 0], bq0.rearrange("(a n) -> a n", a=1).to_broadcast([P, C])),
                    (bias_rows[:, 1], bv0.rearrange("(a n) -> a n", a=1).to_broadcast([P, C])))):
                sp.dma_start(to, of).then_inc(consts_loaded, 16)
            for to, of in ((bo_c, bo0), (bk_c, bk0), (g0_c, gamma0), (b0_c, beta0), (g1_c, gamma1), (b1_c, beta1),
                           (bp_c, bproj1), (bqkv_c, bqkv1)):
                with nc.allow_non_contiguous_dma(reason="a bias column, 2 KB in all"):
                    sp.dma_start(to, column(of)).then_inc(consts_loaded, 16)
            for w in range(2, 4):
                sp.wait_ge(w_lo_done, w - 1)
                sp.dma_start(w32[:, w % 2], rows(weights[w])).then_inc(w_loaded[w % 2], 16)
            with sp.Fori(0, B - 1) as b:
                for h in range(NH):
                    sp.wait_ge(x_lo_done, b * NH + h + 1)
                    cols = slice(h * HALF, (h + 1) * HALF)
                    sp.dma_start(x32[:, :, cols], x_v[b + 1, :, :, cols]).then_inc(x_loaded[h], 16)
                for h in range(NH):
                    sp.wait_ge(y_ready, b * NH * CT + (h + 1) * CT)
                    sp.dma_start(y_v[b, :, :, h * HALF:(h + 1) * HALF], y32[:, h]).then_inc(y_stored[h], 16)
            for h in range(NH):
                sp.wait_ge(y_ready, (B - 1) * NH * CT + (h + 1) * CT)
                sp.dma_start(y_v[B - 1, :, :, h * HALF:(h + 1) * HALF], y32[:, h]).then_inc(y_stored[h], 16)
            for h in range(NH):
                sp.wait_ge(y_stored[h], 16 * B)

            for half in out_stored:
                sp.sem_inc(half, ONE)
            sp.wait_ge(gran_stored, GRAN * 16)

            def pieces(first, n):
                return f(w1_dram[first:first + n].rearrange("g p a j m -> p g (a j m)"))

            def load_stream(slot, first):
                sp.dma_start(f(w_s[:, slot].rearrange("p g a j m -> p g (a j m)")), pieces(first, 2)).then_inc(ws_loaded[slot], 16)

            def load_y(b, us_):
                for u in us_:
                    if u >= 2:
                        sp.wait_ge(xn_lo_done, b * NH * CT + u - 1)
                    src = y_v[b, :, u // NH, u % NH * HALF:(u % NH + 1) * HALF]
                    sp.dma_start(y_half[:, u % 2], src).then_inc(y_half_loaded[u % 2], 16)

            load_stream(1, 0)
            load_y(0, range(NH * CT))
            sp.dma_start(f(w_v1.rearrange("p g a j m -> p g (a j m)")), pieces(3 * CT, CT)).then_inc(wv1_loaded, 16)
            load_stream(0, 2)
            sp.wait_ge(work_full, QK)
            load_stream(1, 4)

            def batch1(b, last):
                sp.wait_ge(work_full, qk_used(b, 0))
                load_stream(0, 6)
                sp.wait_ge(work_full, qk_used(b, 1))
                load_stream(1, 10 if last else 0)
                if not last:
                    load_y(b + 1, range(2))
                if not last:
                    load_y(b + 1, range(2, NH * CT))
                sp.wait_ge(work_full, qk_used(b, 2))
                load_stream(0, 8)
                if not last:
                    sp.wait_ge(work_full, qk_used(b, 3))
                    load_stream(1, 10)
                sp.wait_ge(pv_done, ONE + (b + 1) * PAIRS * NT)
                sp.wait_ge(sum_step, ONE + (b + 1) * PAIRS * 2 * (NT - 1))
                sp.dma_start(res32, y_v[b]).then_inc(res_loaded, 16)
                for o in range(CT):
                    sp.wait_ge(work_free, proj_used(b, (o + 1) * NH, last))
                    sp.dma_start(out_v[b, :, o], res32[:, o]).then_inc(out_stored[o // 2], 16)
                    if not last and o % 2:
                        load_stream(o // 2, 2 + o // 2 * 2)

            with sp.Fori(0, B - 1) as b:
                batch1(b, False)
            batch1(B - 1, True)
            for half in out_stored:
                sp.wait_ge(half, ONE + B * CT // 2 * 16)

        @block.gpsimd
        def _(pool):
            pool.memset(eye_wide, 0.0).then_inc(pool_step, 1)
            pool.memset(eye, 0.0).then_inc(pool_step, 1)
            pool.memset(mask[:, :, :], 0.0).then_inc(pool_step, 1)
            pool.memset(group_avg, 1.0 / GC).then_inc(pool_step, 1)
            pool.memset(ones64, 1.0).then_inc(pool_step, 1)
            pool.memset(f(ms), 0.0).then_inc(pool_step, 1)
            pool.wait_ge(pool_step, 6)
            mid = eye_wide[:, C - P:C]
            pool.affine_select(out=mid, in_=mid, compare_op=ALU.not_equal, fill=1.0, base=0,
                               pattern=[[-1, P]], channel_multiplier=1).then_inc(pool_step, 1)
            pool.wait_ge(pool_step, 7)
            pool.affine_select(out=eye, in_=eye, compare_op=ALU.not_equal, fill=1.0, base=0,
                               pattern=[[-1, P]], channel_multiplier=1).then_inc(pool_step, 1)
            for h in range(2):
                pool.wait_ge(pool_step, 8 + h)
                pool.affine_select(out=mask[32 * h:32 * h + 32, :, :], in_=mask[32 * h:32 * h + 32, :, :],
                                   compare_op=ALU.not_equal, fill=-1.0, base=0,
                                   pattern=[[-1, NT], [0, P]], channel_multiplier=1).then_inc(pool_step, 1)
            blocks = group_avg.rearrange("p (g c) -> p g c", c=GC)
            pool.wait_ge(pool_step, 10)
            pool.affine_select(out=blocks, in_=blocks, compare_op=ALU.is_ge, fill=0.0, base=0,
                               pattern=[[-GC, P // GC], [0, GC]], channel_multiplier=1).then_inc(pool_step, 1)
            pool.wait_ge(pool_step, 11)
            pool.affine_select(out=blocks, in_=blocks, compare_op=ALU.is_ge, fill=0.0, base=GC - 1,
                               pattern=[[GC, P // GC], [0, GC]], channel_multiplier=-1).then_inc(pool_step, 1)
            pool.wait_ge(pool_step, 12)
            pool.sem_inc(consts_ready, 1)
            with pool.Fori(0, GRAN) as g:
                pool.dma_start(gran32, w1[g]).then_inc(gran_loaded, 16)
                pool.wait_ge(gran_loaded, g * 16 + 16)
                pool.tensor_tensor(gran_s[:, HI], gran32, ones64[:, 0:1].unsqueeze(1).to_broadcast([P, CT, P]), ALU.mult).then_inc(gran_split, 1)
                pool.wait_ge(gran_split, g * 2 + 1)
                pool.tensor_tensor(gran_s[:, LO], gran32, f(gran_s[:, HI]), ALU.subtract).then_inc(gran_split, 1)
                pool.wait_ge(gran_split, g * 2 + 2)
                pool.dma_start(w1_dram[g], gran_s).then_inc(gran_stored, 16)
                pool.wait_ge(gran_stored, g * 16 + 16)

            pool.sem_inc(sum_step, ONE)
            pool.wait_ge(y_full, B * NH * CT)
            n = 0
            for h in range(2):
                pad = slice(D - h * D, 2 * D - h * D)
                pick = slice(D - h * D, D - h * D + NT)
                for to, value in ((q_b[pad, h], 0.0), (k_b[pad, 0, h], 0.0), (k_b[pad, 1, h], 0.0),
                                  (k_b[pick, 0, h], 1.0), (k_b[pick, 1, h], 1.0)):
                    if n:
                        pool.wait_ge(pads_ready, n)
                    pool.memset(f(to), value).then_inc(pads_ready, 1)
                    n += 1

            def batch1(b, last):
                for p in range(PAIRS):
                    for i in range(1, NT):
                        for h in range(2):
                            if i == 1 and h == 0:
                                pool.wait_ge(work_full, sums_used(b, p, last))
                            pool.wait_ge(probs_ready, ONE + b * PAIRS * 2 * NT + p * 2 * NT + 2 * i + h + 1)
                            pool.wait_ge(sum_step, ONE + b * PAIRS * 2 * (NT - 1) + p * 2 * (NT - 1) + 2 * (i - 1) + h)
                            pool.tensor_tensor(p_sum[:, h], probs[:, 0, h] if i == 1 else p_sum[:, h],
                                               probs[:, i % 2, h], ALU.add).then_inc(sum_step, 1)

            with pool.Fori(0, B - 1) as b:
                batch1(b, False)
            batch1(B - 1, True)

        @block.scalar
        def _(act):
            for w, to in enumerate((w_q, w_v)):
                act.wait_ge(w_loaded[w], 16)
                act.activation(to[:, HI], w32[:, w], ACT.Copy).then_inc(w_hi_done, 1)

            def later_weights():
                for w, to in ((2, w_k), (3, w_o)):
                    act.wait_ge(w_loaded[w % 2], 32)
                    act.activation(to[:, HI], w32[:, w % 2], ACT.Copy).then_inc(w_hi_done, 1)

            def batch(b, first):
                for h in range(NH):
                    cols = slice(h * HALF, (h + 1) * HALF)
                    act.wait_ge(x_loaded[h], b * 16 + 16)
                    if not first:
                        act.wait_ge(y_full, b * NH * CT - CT * (NH - 1 - h))
                    act.activation(xs[:, HI, :, cols], x32[:, :, cols], ACT.Copy).then_inc(x_hi_done, 1)
                if first:
                    later_weights()
                for t in range(KV):
                    act.wait_ge(ring_free, b * FREE0 + t + 1)
                    if t // 2 < 2:
                        act.wait_ge(m_full, b * CT)
                    else:
                        act.wait_ge(kv_used, b * (NT - 1) + t // 2 - 1)
                    act.activation((ks, vs)[t % 2][:, t // 2 % 2, HI], kv32[:, t % 2], ACT.Copy).then_inc(hi_done, 1)
                for g in range(CT):
                    act.wait_ge(ring_full, b * RING0 + U0 + g + 1)
                    act.activation(us[:, HI, g], ring_bank(U0 + g), ACT.Copy).then_inc(hi_done, 1)
                for g in range(CT):
                    act.wait_ge(ring_free, b * FREE0 + KV + g + 1)
                    act.activation(a_s[:, HI, g], kv32[:, g % 2], ACT.Copy).then_inc(hi_done, 1)
                act.wait_ge(c_ready, b + 1)
                for h in range(NH):
                    act.wait_ge(y_stored[h], b * 16)
                    act.wait_ge(y_counted, b * NH * CT)
                    for o in range(CT):
                        act.wait_ge(y_full, b * NH * CT + h * CT + o + 1)
                        act.activation(y32[:, h, o], bank(o), ACT.Identity, bias=c_vec[:, o:o + 1]).then_inc(y_ready, 1)

            batch(0, True)
            with act.Fori(1, B) as b:
                batch(b, False)

            work = Tally()

            def norm_half(b, u):
                j, cols = u // NH, slice(u % NH * HALF, (u % NH + 1) * HALF)
                act.wait_ge(xn_made, b * NH * CT + u + 1)
                act.activation(xn[:, HI, j, cols], y_half[:, u % 2], ACT.Copy).then_inc(xn_hi_done, 1)

            def qk_hi(b, pair, par, i, count):
                n, ps = work.next()
                act.wait_ge(work_full, n)
                of_k, cols = i // 2, slice(i % 2 * HALF, (i % 2 + 1) * HALF)
                bias = bqkv_c[:, of_k * CT + pair:of_k * CT + pair + 1]
                to = (q_a, k_a)[of_k]
                for h in range(2):
                    rows_ = slice(h * D, h * D + D)
                    act.activation(to[rows_, par, h, cols], ps[rows_, :], ACT.Identity, bias=bias[rows_]).then_inc(qk_hi_done, 1)
                if of_k:
                    act.wait_ge(qk_hi_done, 2 * (count + i + 1))
                    for h in range(2):
                        rows_, others = slice(h * D, h * D + D), slice(D - h * D, 2 * D - h * D)
                        act.activation(k_a[others, par, h, cols], f(k_a[rows_, par, h, cols]), ACT.Copy).then_inc(k_twice, 1)

            def q_b_hi(par):
                for h in range(2):
                    rows_ = slice(h * D, h * D + D)
                    act.activation(q_b[rows_, h], f(q_a[rows_, par, h]), ACT.Copy).then_inc(q_b_ready, 1)

            def hid_hi(b, pair, h):
                cols = slice(h * HALF, (h + 1) * HALF)
                act.wait_ge(o_normed, ONE + b * PAIRS * NH + pair * NH + h + 1)
                act.activation(hid[:, HI, pair, cols], o32[:, cols], ACT.Identity,
                               bias=bqkv_c[:, 2 * CT + pair:2 * CT + pair + 1]).then_inc(hid_hi_done, 1)

            for i, (v, root) in enumerate(((bn_var, bn_scale), (gn_in, gn_tmp))):
                act.wait_ge(var_ready, i + 1)
                act.activation(root, v, ACT.Sqrt).then_inc(root_ready, 1)
            act.sem_inc(probs_ready, ONE)
            act.sem_inc(o_ready, ONE)
            act.wait_ge(norm_ready, 1)
            for u in range(NH * CT):
                norm_half(0, u)
            for i in range(QK):
                qk_hi(0, 0, 0, i, 0)
            q_b_hi(0)

            def batch1(b, last):
                work.start(b)
                for p in range(PAIRS):
                    more = p < PAIRS - 1 or not last
                    par, pairs = (p + 1) % 2, b * PAIRS + p

                    def next_qk(i):
                        if more:
                            qk_hi(b, (p + 1) % PAIRS, par, i, (pairs + 1) * QK)

                    next_qk(0)
                    for i in range(NT):
                        for h in range(2):
                            act.wait_ge(scores_full, pairs * 2 * NT + 2 * i + h + 1)
                            if h == 0 and i >= 2:
                                act.wait_ge(pv_done, ONE + pairs * NT + i - 1)
                            if i >= 2:
                                act.wait_ge(sum_step, ONE + pairs * 2 * (NT - 1) + 2 * (max(i - 2, 1) - 1) + h + 1)
                            elif p == 0 and h == 0:
                                if i == 0:
                                    act.wait_ge(sum_step, ONE + pairs * 2 * (NT - 1))
                                    act.wait_ge(pv_done, ONE + pairs * NT)
                                act.wait_ge(out_stored[i], ONE + b * CT // 2 * 16)
                            elif p:
                                act.wait_ge(sum_step, ONE + pairs * 2 * (NT - 1) - 2 * (1 - i) - 1 + h)
                            act.activation(probs[:, i % 2, h], psum[h][:, :, :].rearrange("p a n -> p (a n)"), ACT.Exp,
                                           scale=SCALE).then_inc(probs_ready, 1)
                        if p and i < NH:
                            work.next()
                        if i == 0:
                            next_qk(1)
                        if i == 1:
                            next_qk(2)
                            if p:
                                hid_hi(b, p - 1, 0)
                            next_qk(3)
                            if p:
                                hid_hi(b, p - 1, 1)
                        if more:
                            for _ in range(ROWS[i]):
                                work.next()
                        if p == 2 and not last:
                            if i == 1:
                                act.wait_ge(work_full, qk_used(b, 2))
                                for u in range(2):
                                    norm_half(b + 1, u)
                            for u in range(NH * CT):
                                if sum(ROWS[:i]) <= NORM_ROW[u] < sum(ROWS[:i + 1]):
                                    norm_half(b + 1, u)
                    if more:
                        work.next()
                        q_b_hi(par)
                    act.wait_ge(hid_lo_done, ONE + pairs * NH)
                    act.wait_ge(pv_done, ONE + (pairs + 1) * NT)
                    act.activation(o32, psum[2][:, :, :].rearrange("p a n -> p (a n)"), ACT.Copy).then_inc(o_ready, 1)
                for h in range(NH):
                    hid_hi(b, PAIRS - 1, h)
                act.wait_ge(res_loaded, (b + 1) * 16)
                for o in range(CT):
                    act.activation(res32[:, o], res32[:, o], ACT.Identity, scale=bn_scale[:, o:o + 1],
                                   bias=res_bias[:, o:o + 1]).then_inc(res_scaled, 1)

            with act.Fori(0, B - 1) as b:
                batch1(b, False)
            batch1(B - 1, True)

        @block.vector
        def _(dve):
            def split_w(w, to):
                dve.wait_ge(w_hi_done, w + 1)
                dve.tensor_tensor(to[:, LO], w32[:, w % 2], f(to[:, HI]), ALU.subtract).then_inc(w_lo_done, 1)

            split_w(0, w_q)
            split_w(1, w_v)
            dve.wait_ge(consts_loaded, 10 * 16)
            dve.tensor_copy(bk_s[:, :, HI], bk_c).then_inc(dve_step, 1)
            dve.wait_ge(dve_step, 1)
            dve.tensor_tensor(bk_s[:, :, LO], bk_c, f(bk_s[:, :, HI]), ALU.subtract).then_inc(dve_step, 1)
            dve.wait_ge(consts_ready, 1)
            FIRST, STEPS = 2, 4 * CT // 2 + 1

            def batch(b, first):
                for h in range(NH):
                    cols = slice(h * HALF, (h + 1) * HALF)
                    dve.wait_ge(x_hi_done, b * NH + h + 1)
                    dve.tensor_tensor(xs[:, LO, :, cols], x32[:, :, cols], f(xs[:, HI, :, cols]),
                                      ALU.subtract).then_inc(x_lo_done, 1)
                if first:
                    split_w(2, w_k)
                    split_w(3, w_o)

                def kv_lo(t):
                    dve.wait_ge(hi_done, b * RING0 + t + 1)
                    to = (ks, vs)[t % 2][:, t // 2 % 2]
                    dve.tensor_tensor(to[:, LO], kv32[:, t % 2], f(to[:, HI]), ALU.subtract).then_inc(lo_done, 1)

                for t in range(KV):
                    dve.wait_ge(ring_full, b * RING0 + t + 1)
                    dve.wait_ge(lo_done, b * RING0 + max(0, t - 1))
                    dve.tensor_tensor(kv32[:, t % 2], ring_bank(t), bias_rows[:, t % 2], ALU.add).then_inc(ring_free, 1)
                    if t:
                        kv_lo(t - 1)
                kv_lo(KV - 1)
                for g in range(CT):
                    dve.wait_ge(m_full, b * CT + g + 1)
                    if g == 0:
                        dve.wait_ge(m_split, b * 2 * CT)
                    for e in range(2):
                        part = slice(e * D, e * D + D)
                        of = bank(g)[part, g % 2 * P + e * D:g % 2 * P + e * D + D]
                        dve.tensor_copy(ms[part, HI, g, part], of).then_inc(dve_step, 1)
                    dve.wait_ge(dve_step, b * STEPS + FIRST + 2 * g + 2)
                    for e in range(2):
                        part = slice(e * D, e * D + D)
                        of = bank(g)[part, g % 2 * P + e * D:g % 2 * P + e * D + D]
                        dve.tensor_tensor(ms[part, LO, g, part], of, f(ms[part, HI, g, part]),
                                          ALU.subtract).then_inc(m_split, 1)
                for g in range(CT):
                    dve.wait_ge(hi_done, b * RING0 + U0 + g + 1)
                    dve.tensor_tensor(us[:, LO, g], ring_bank(U0 + g), f(us[:, HI, g]), ALU.subtract).then_inc(lo_done, 1)

                def a_lo(g):
                    dve.wait_ge(hi_done, b * RING0 + A0 + g + 1)
                    dve.tensor_tensor(a_s[:, LO, g], kv32[:, g % 2], f(a_s[:, HI, g]), ALU.subtract).then_inc(lo_done, 1)

                for g in range(CT):
                    dve.wait_ge(ring_full, b * RING0 + A0 + g + 1)
                    dve.wait_ge(lo_done, b * RING0 + A0 + max(0, g - 1))
                    dve.tensor_tensor(kv32[:, g % 2], ring_bank(A0 + g), eye_wide[:, C - P - g * P:2 * C - P - g * P],
                                      ALU.add).then_inc(ring_free, 1)
                    if g:
                        a_lo(g - 1)
                a_lo(CT - 1)
                dve.wait_ge(c_full, b + 1)
                dve.wait_ge(c_ready, b)
                dve.reduce_sum(c_sum, bank(3)[:, 0:2 * CT].rearrange("p (o t) -> p o t", t=2), AX_X).then_inc(dve_step, 1)
                dve.wait_ge(dve_step, b * STEPS + FIRST + STEPS)
                dve.wait_ge(y_ready, b * NH * CT)
                dve.tensor_tensor(c_vec, c_sum, bo_c, ALU.add).then_inc(c_ready, 1)
                for h in range(NH):
                    for o in range(CT):
                        dve.wait_ge(y_ready, b * NH * CT + h * CT + o + 1)
                        if first:
                            to = stats[:, o, h, :]
                        else:
                            to = stats[:, o, bass.ds(b * NH + h, 1), :].rearrange("p a k -> p (a k)")
                        dve.bn_stats(to, y32[:, h, o]).then_inc(y_counted, 1)

            batch(0, True)
            with dve.Fori(1, B) as b:
                batch(b, False)

            steps = FIRST + B * STEPS

            def then(ins):
                nonlocal steps
                steps += 1
                ins.then_inc(dve_step, 1)
                dve.wait_ge(dve_step, steps)

            def invert(root, v, tmp):
                then(dve.reciprocal(root, root))
                then(dve.tensor_tensor(tmp, root, root, ALU.mult))
                then(dve.tensor_tensor(tmp, tmp, v, ALU.mult))
                then(dve.tensor_scalar(tmp, tmp, -0.5, 1.5, ALU.mult, ALU.add))
                then(dve.tensor_tensor(root, root, tmp, ALU.mult))

            def wide(v):
                return v.unsqueeze(2).to_broadcast([P, CT, B])

            dve.wait_ge(y_counted, B * NH * CT)
            for j in range(CT):
                dve.bn_aggr(bn_mv[:, j], stats[:, j].rearrange("p a k -> p (a k)")).then_inc(dve_step, 1)
                for b in range(B):
                    dve.bn_aggr(mean_var[:, j, b], stats[:, j, b * NH:(b + 1) * NH].rearrange("p a k -> p (a k)")).then_inc(dve_step, 1)
            steps += CT * (B + 1)
            dve.wait_ge(dve_step, steps)
            dve.tensor_scalar(bn_var, bn_mv[:, :, 1], EPS, None, ALU.add).then_inc(var_ready, 1)
            dve.wait_ge(root_ready, 1)
            invert(bn_scale, bn_var, root_tmp[:, 0:CT])
            then(dve.tensor_tensor(bn_scale, bn_scale, g0_c, ALU.mult))
            then(dve.tensor_tensor(bn_bias, bn_mv[:, :, 0], bn_scale, ALU.mult))
            then(dve.tensor_tensor(bn_bias, b0_c, bn_bias, ALU.subtract))
            then(dve.tensor_tensor(res_bias, bn_bias, bp_c, ALU.add))
            then(dve.tensor_tensor(x1_mean, mean_var[:, :, :, 0], wide(bn_scale), ALU.mult))
            dve.tensor_tensor(x1_mean, x1_mean, wide(bn_bias), ALU.add).then_inc(gn_moved, 1)
            dve.wait_ge(gn_moved, 1)
            dve.wait_ge(gn_averaged, 1)
            then(dve.tensor_copy(gn_mean, bank(6)[:, 0:CT * B].rearrange("p (j b) -> p j b", b=B)))
            then(dve.tensor_tensor(gn_tmp, x1_mean, gn_mean, ALU.subtract))
            then(dve.tensor_tensor(gn_tmp, gn_tmp, gn_tmp, ALU.mult))
            then(dve.tensor_tensor(gn_in, mean_var[:, :, :, 1], wide(bn_scale), ALU.mult))
            then(dve.tensor_tensor(gn_in, gn_in, wide(bn_scale), ALU.mult))
            dve.tensor_tensor(gn_in, gn_in, gn_tmp, ALU.add).then_inc(gn_moved, 1)
            dve.wait_ge(gn_averaged, 2)
            dve.tensor_scalar(gn_in, bank(7)[:, 0:CT * B].rearrange("p (j b) -> p j b", b=B), EPS, None, ALU.add).then_inc(var_ready, 1)
            dve.wait_ge(root_ready, 2)
            invert(gn_tmp, gn_in, root_tmp.rearrange("p (j b) -> p j b", b=B))
            then(dve.tensor_tensor(gn_tmp, gn_tmp, wide(g1_c), ALU.mult))
            then(dve.tensor_tensor(xn_scale, gn_tmp, wide(bn_scale), ALU.mult))
            then(dve.tensor_tensor(xn_bias, wide(bn_bias), gn_mean, ALU.subtract))
            then(dve.tensor_tensor(xn_bias, xn_bias, gn_tmp, ALU.mult))
            then(dve.memset(max_cols, 0.0))
            dve.tensor_tensor(xn_bias, xn_bias, wide(b1_c), ALU.add).then_inc(norm_ready, 1)

            work = Tally()

            def norm(b, u):
                dve.wait_ge(y_half_loaded[u % 2], b * (NH * CT // 2 * 16) + (u // 2 + 1) * 16)
                at = [v[:, u // NH, bass.ds(b, 1)] for v in (xn_scale, xn_bias)]
                dve.tensor_scalar(y_half[:, u % 2], y_half[:, u % 2], at[0], at[1], ALU.mult, ALU.add).then_inc(xn_made, 1)

            def norm_lo(b, u):
                j, cols = u // NH, slice(u % NH * HALF, (u % NH + 1) * HALF)
                dve.wait_ge(xn_hi_done, b * NH * CT + u + 1)
                dve.tensor_tensor(xn[:, LO, j, cols], y_half[:, u % 2], f(xn[:, HI, j, cols]), ALU.subtract).then_inc(xn_lo_done, 1)

            def qk_lo(pair, par, i, count):
                n, ps = work.next()
                dve.wait_ge(qk_hi_done, 2 * (count + i + 1))
                of_k, cols = i // 2, slice(i % 2 * HALF, (i % 2 + 1) * HALF)
                bias = bqkv_c[:, of_k * CT + pair:of_k * CT + pair + 1]
                for h in range(2):
                    rows_, others = slice(h * D, h * D + D), slice(D - h * D, 2 * D - h * D)
                    to = k_b[rows_, par, h, cols] if of_k else q_a[others, par, h, cols]
                    ins = dve.scalar_tensor_tensor(out=to, in0=ps[rows_, :], scalar=bias[rows_],
                                                   in1=f((q_a, k_a)[of_k][rows_, par, h, cols]),
                                                   op0=ALU.add, op1=ALU.subtract)
                ins.then_inc(work_free, 1)

            def max_tile(t):
                n, ps = work.next()
                h, tile, half = t // (NT * NH), t // NH % NT, t % NH
                dve.wait_ge(work_full, n)
                dve.reduce_max(max2[:, h, tile, half:half + 1], ps, AX_X).then_inc(work_free, 1)

            def max_join():
                dve.wait_ge(work_free, work.upto())
                dve.tensor_tensor(max_cols[:, 0:2, 0:NT], max2[:, :, :, 0], max2[:, :, :, 1], ALU.max).then_inc(max_ready, 1)

            def max_rows(pairs):
                n, ps = work.next()
                dve.wait_ge(work_full, n)
                dve.wait_ge(scores_full, pairs * 2 * NT)
                for h in range(2):
                    of = ps[32 * h:32 * h + NT, 0:P].unsqueeze(1).to_broadcast([NT, NT, P])
                    to = q_b[D - h * D:D - h * D + NT, h].rearrange("p (j t) -> p j t", j=NT)
                    ins = dve.tensor_tensor(to, of, mask[32 * h:32 * h + NT, :, :], ALU.mult)
                ins.then_inc(work_free, 1)

            def v_tile(b, i):
                n, ps = work.next()
                dve.wait_ge(work_full, n)
                if i == 0:
                    dve.wait_ge(pv_done, ONE + b * PAIRS * NT)
                dve.tensor_copy(v_t[:, i], ps).then_inc(work_free, 1)

            def normalise(b, pair, h):
                n, ps = work.next()
                cols, halves = slice(h * HALF, (h + 1) * HALF), b * PAIRS * NH + pair * NH + h
                dve.wait_ge(work_full, n)
                dve.wait_ge(o_normed, ONE + halves)
                dve.reciprocal(recip, ps).then_inc(work_free, 1)
                if h == 0:
                    dve.wait_ge(o_ready, ONE + b * PAIRS + pair + 1)
                dve.wait_ge(work_free, n)
                dve.tensor_tensor(o32[:, cols], o32[:, cols], recip, ALU.mult).then_inc(o_normed, 1)

            def hid_lo(b, pair, h):
                cols = slice(h * HALF, (h + 1) * HALF)
                dve.wait_ge(hid_hi_done, b * PAIRS * NH + pair * NH + h + 1)
                dve.scalar_tensor_tensor(out=hid[:, LO, pair, cols], in0=o32[:, cols],
                                         scalar=bqkv_c[:, 2 * CT + pair:2 * CT + pair + 1],
                                         in1=f(hid[:, HI, pair, cols]), op0=ALU.add, op1=ALU.subtract).then_inc(hid_lo_done, 1)

            dve.sem_inc(hid_lo_done, ONE)
            dve.sem_inc(o_normed, ONE)
            dve.wait_ge(pads_ready, 10)
            dve.wait_ge(norm_ready, 1)
            norm(0, 0)
            for u in range(1, NH * CT + 1):
                if u < NH * CT:
                    norm(0, u)
                norm_lo(0, u - 1)
            for i in range(QK):
                qk_lo(0, 0, i, 0)
            for t in range(SMAX):
                max_tile(t)
            max_join()
            max_rows(0)
            for i in range(NT):
                v_tile(0, i)

            def batch1(b, last):
                work.start(b)
                for p in range(PAIRS):
                    more = p < PAIRS - 1 or not last
                    par, pairs = (p + 1) % 2, b * PAIRS + p

                    def next_qk(i):
                        if more:
                            qk_lo((p + 1) % PAIRS, par, i, (pairs + 1) * QK)

                    next_qk(0)
                    if p:
                        normalise(b, p - 1, 0)
                    next_qk(1)
                    if p:
                        normalise(b, p - 1, 1)
                    next_qk(2)
                    if p:
                        hid_lo(b, p - 1, 0)
                    if p == 2 and not last:
                        for u in range(2):
                            norm(b + 1, u)
                    next_qk(3)
                    if p:
                        hid_lo(b, p - 1, 1)
                    if more:
                        dve.wait_ge(max_ready, pairs + 1)
                        for t in range(SMAX):
                            if p == 2 and not last:
                                for u in range(NH * CT):
                                    if NORM_ROW[u] == t:
                                        norm(b + 1, u)
                                for u in range(NH * CT):
                                    if LO_ROW[u] == t:
                                        norm_lo(b + 1, u)
                            max_tile(t)
                        max_join()
                        max_rows(pairs + 1)
                for i in range(NT):
                    if not last:
                        v_tile(b + 1, i)
                    if i in (2, 4):
                        normalise(b, PAIRS - 1, i // 2 - 1)
                    if i in (5, 6):
                        hid_lo(b, PAIRS - 1, i - 5)
                for t in range(CT * NH):
                    n, ps = work.next()
                    o, cols = t // NH, slice(t % NH * HALF, (t % NH + 1) * HALF)
                    dve.wait_ge(work_full, n)
                    dve.wait_ge(res_scaled, b * CT + o + 1)
                    dve.tensor_tensor(res32[:, o, cols], ps, res32[:, o, cols], ALU.add).then_inc(work_free, 1)

            with dve.Fori(0, B - 1) as b:
                batch1(b, False)
            batch1(B - 1, True)

        @block.tensor
        def _(pe):
            def product(to, pairs):
                for i, (w, m) in enumerate(pairs):
                    last = pe.matmul(to, w, m, start=(i == 0), stop=(i == len(pairs) - 1))
                return last

            def batch(b, first):
                def m_products(n):
                    pe.wait_ge(lo_done, b * RING0 + 2 * n + 2)
                    if n == 0:
                        pe.wait_ge(y_ready, b * NH * CT)
                    for g in range(CT):
                        window = slice(g // 2 * 2 * P, (g // 2 + 1) * 2 * P)
                        for i, (v, k) in enumerate(THREE):
                            last = pe.matmul(bank(g)[:, 0:2 * P], vs[:, n % 2, v, g * P:(g + 1) * P],
                                             ks[:, n % 2, k, window], start=(n == 0 and i == 0),
                                             stop=(n == NT - 1 and i == 2))
                        if n == NT - 1:
                            last.then_inc(m_full, 1)
                        elif g == CT - 1:
                            last.then_inc(kv_used, 1)

                if first:
                    pe.wait_ge(w_lo_done, 2)
                for n in range(NT):
                    if n % (NT // NH) == 0:
                        pe.wait_ge(x_lo_done, b * NH + n // (NT // NH) + 1)
                    for which, w in enumerate((w_q, w_v)):
                        t = 2 * n + which
                        pe.wait_ge(ring_free, b * FREE0 + max(0, t - 3))
                        product(ring_bank(t), [(xs[:, i, j, n * P:(n + 1) * P], w[:, k, j])
                                               for j in range(CT) for i, k in THREE]).then_inc(ring_full, 1)
                    if n:
                        m_products(n - 1)
                m_products(NT - 1)
                if first:
                    pe.wait_ge(w_lo_done, 4)
                for g in range(CT):
                    pe.wait_ge(m_split, b * 2 * CT + 2 * g + 2)
                    if g == 0:
                        pe.wait_ge(ring_free, b * FREE0 + KV)
                    product(ring_bank(U0 + g), [(ms[:, i, g], w_o[:, k, g]) for i, k in THREE]).then_inc(ring_full, 1)
                pe.wait_ge(lo_done, b * RING0 + U0 + CT)
                for g in range(CT):
                    product(ring_bank(A0 + g), [(w_k[:, i, j, g * P:(g + 1) * P], us[:, k, j])
                                                for j in range(CT) for i, k in THREE]).then_inc(ring_full, 1)
                for o in range(CT):
                    last = product(bank(3)[:, 2 * o:2 * o + 2], [(us[:, i, j, o * P:(o + 1) * P], bk_s[:, j])
                                                                 for j in range(CT) for i in (HI, LO)])
                last.then_inc(c_full, 1)
                pe.wait_ge(lo_done, b * RING0 + RING0)
                for h in range(NH):
                    for o in range(CT):
                        i = h * CT + o
                        if i == 3:
                            pe.wait_ge(c_ready, b + 1)
                        if i >= CT:
                            pe.wait_ge(y_ready, b * NH * CT + i - CT + 1)
                        product(bank(o), [(a_s[:, w, j, o * P:(o + 1) * P], xs[:, m, j, h * HALF:(h + 1) * HALF])
                                          for j in range(CT) for w, m in THREE]).then_inc(y_full, 1)

            batch(0, True)
            with pe.Fori(1, B) as b:
                batch(b, False)

            for i, of in enumerate((x1_mean, gn_in)):
                pe.wait_ge(gn_moved, i + 1)
                pe.matmul(bank(6 + i)[:, 0:CT * B], group_avg, of.rearrange("p j b -> p (j b)"),
                          start=True, stop=True).then_inc(gn_averaged, 1)
            work = Tally()

            def next_tile():
                n, ps = work.next()
                if work.started or work.n > 2:
                    pe.wait_ge(work_free, n - 2)
                return ps

            def qk_tile(slot, i):
                piece, cols = i // 2, slice(i % 2 * HALF, (i % 2 + 1) * HALF)
                product(next_tile(), [(w_s[:, slot, piece, w, j], xn[:, m, j, cols])
                                      for j in range(CT) for w, m in THREE]).then_inc(work_full, 1)

            def max_tile(par, t):
                h, tile, half = t // (NT * NH), t // NH % NT, t % NH
                pe.matmul(next_tile(), q_a[:, par, h, tile * P:(tile + 1) * P],
                          k_a[:, par, h, half * HALF:(half + 1) * HALF], start=True, stop=True).then_inc(work_full, 1)

            def max_turn(pairs):
                pe.wait_ge(max_ready, pairs + 1)
                pe.transpose(next_tile()[:, 0:P], max_cols.rearrange("p h t -> p (h t)"), eye).then_inc(work_full, 1)

            def v_tile(i):
                product(next_tile(), [(xn[:, m, j, i * P:(i + 1) * P], w_v1[:, :, w, j])
                                      for j in range(CT) for w, m in THREE]).then_inc(work_full, 1)

            def scores(pairs, par, i, between):
                for h in range(2):
                    pe.wait_ge(probs_ready, ONE + pairs * 2 * NT + 2 * max(i - 1, 0) + (h + 1 if i else 0))
                    keys = slice(i * P, (i + 1) * P)
                    for first, (k, q) in ((True, (k_a[:, par, h, keys], q_a[:, par, h])), (False, (k_b[:, par, h, keys], q_b[:, h]))):
                        for half in range(NH):
                            last = pe.matmul(psum[h][:, half], k, q[:, half * HALF:(half + 1) * HALF], start=first, stop=not first)
                        if not first:
                            last.then_inc(scores_full, 1)
                        between(2 * h + (not first))

            def weigh(b, p, i, between):
                pairs = b * PAIRS + p
                pe.wait_ge(probs_ready, ONE + pairs * 2 * NT + 2 * i + 2)
                if i == 0:
                    pe.wait_ge(o_ready, ONE + pairs)
                for half in range(NH):
                    for h in range(2):
                        head = slice((2 * p + h) * D, (2 * p + h + 1) * D)
                        last = pe.matmul(psum[2][h * D:(h + 1) * D, half], v_t[:, i, head],
                                         probs[:, i % 2, h, half * HALF:(half + 1) * HALF], start=(i == 0), stop=(i == NT - 1))
                    if half == NH - 1:
                        last.then_inc(pv_done, 1)
                    between(4 + half)

            def sums(pairs, half):
                ps = next_tile()
                pe.wait_ge(sum_step, ONE + (pairs + 1) * 2 * (NT - 1))
                for h in range(2):
                    last = pe.matmul(ps[h * D:(h + 1) * D, :], ones64, p_sum[:, h, half * HALF:(half + 1) * HALF],
                                     start=True, stop=True)
                last.then_inc(work_full, 1)

            pe.sem_inc(pv_done, ONE)
            pe.wait_ge(xn_lo_done, NH * CT)
            pe.wait_ge(ws_loaded[1], 16)
            for i in range(QK):
                qk_tile(1, i)
            pe.wait_ge(k_twice, QK)
            pe.wait_ge(work_free, QK)
            for t in range(SMAX):
                max_tile(0, t)
            max_turn(0)
            pe.wait_ge(wv1_loaded, 16)
            for i in range(NT):
                v_tile(i)
            pe.wait_ge(work_free, WORK0)

            def batch1(b, last):
                work.start(b)
                loads = b * ((PAIRS + 2) // 2)
                for p in range(PAIRS):
                    more = p < PAIRS - 1 or not last
                    par, pairs = p % 2, b * PAIRS + p
                    def next_qk(i):
                        if more:
                            if i == 0:
                                slot = p % 2
                                pe.wait_ge(ws_loaded[slot], (loads + p // 2 + 1 + slot) * 16)
                                if p == PAIRS - 1:
                                    pe.wait_ge(xn_lo_done, (b + 2) * NH * CT)
                            qk_tile(p % 2, i)

                    next_qk(0)
                    for i in range(NT):
                        def next_row(slot):
                            if more and PLACE0[i] <= slot < PLACE0[i] + ROWS[i]:
                                if i == 2 and slot == PLACE0[i]:
                                    pe.wait_ge(work_free, work.upto())
                                    pe.wait_ge(k_twice, (pairs + 2) * QK)
                                max_tile(1 - par, sum(ROWS[:i]) + slot - PLACE0[i])

                        if i == 0:
                            pe.wait_ge(q_b_ready, 2 * pairs + 2)
                            pe.wait_ge(work_free, work.upto(1 if more else 0))
                        scores(pairs, par, i, next_row)
                        if p and i < NH:
                            sums(pairs - 1, i)
                        if i == 0:
                            next_qk(1)
                        if i == 1:
                            next_qk(2)
                        if i:
                            weigh(b, p, i - 1, next_row)
                        if i == 1:
                            next_qk(3)
                        next_row(6)
                    if more:
                        max_turn(pairs + 1)
                    weigh(b, p, NT - 1, lambda slot: None)
                for i in range(NT):
                    if not last:
                        v_tile(i)
                    if i in (2, 4):
                        sums(b * PAIRS + PAIRS - 1, i // 2 - 1)
                pe.wait_ge(hid_lo_done, ONE + (b + 1) * PAIRS * NH)
                for t in range(CT * NH):
                    o, cols = t // NH, slice(t % NH * HALF, (t % NH + 1) * HALF)
                    slot, piece = o // 2, o % 2
                    if t % (2 * NH) == 0:
                        n_load = (loads + 3 + slot) - (1 if last and slot else 0)
                        pe.wait_ge(ws_loaded[slot], n_load * 16)
                    product(next_tile(), [(w_s[:, slot, piece, w, j], hid[:, m, j, cols])
                                          for j in range(CT) for w, m in THREE]).then_inc(work_full, 1)

            with pe.Fori(0, B - 1) as b:
                batch1(b, False)
            batch1(B - 1, True)



def kernel(**inputs):
    import numpy as _np
    import concourse.bacc as _bacc
    from concourse import mybir as _mybir
    from concourse.bass_utils import run_bass_kernel_spmd as _run

    a = {k: _np.asarray(v) for k, v in inputs.items()}
    qkv, proj = a["L1_conv_w_qkv"], a["L1_conv_w_proj"]
    order = [qkv[i * C + p * P:i * C + (p + 1) * P] for p in range(CT) for i in range(2)]
    order += [proj[p * P:(p + 1) * P] for p in range(CT)]
    order += [qkv[2 * C + p * P:2 * C + (p + 1) * P] for p in range(CT)]
    w1 = _np.stack([w.T.reshape(CT, P, P).transpose(1, 0, 2) for w in order])
    host = {
        "x": a["x"].reshape(B, C, N),
        "wq_t": a["L0_conv_Wq"].T, "wv_t": a["L0_conv_Wv"].T, "wk": a["L0_conv_Wk"], "wo_t": a["L0_conv_Wo"].T,
        "bq0": a["L0_conv_bq"], "bv0": a["L0_conv_bv"], "bk0": a["L0_conv_bk"], "bo0": a["L0_conv_bo"],
        "gamma0": a["L0_conv_gamma"], "beta0": a["L0_conv_beta"],
        "gamma1": a["L1_conv_gamma"], "beta1": a["L1_conv_beta"],
        "w1": w1, "bqkv1": a["L1_conv_b_qkv"], "bproj1": a["L1_conv_b_proj"],
    }
    nc = _bacc.Bacc("TRN2", target_bir_lowering=False, num_devices=1)
    arrays, args = {}, []
    for name, v in host.items():
        v = _np.ascontiguousarray(v)
        arrays[name] = v
        args.append(nc.dram_tensor(name, v.shape, _mybir.dt.from_np(v.dtype), kind="ExternalInput").ap())
    args.append(nc.dram_tensor("out", (B, C, N), F32, kind="ExternalOutput").ap())
    build(nc, *args)
    r = _run(nc, [arrays], core_ids=[0])
    return r.results[0]["out"].reshape(B, C, 32, 32)
```

```python
from contextlib import ExitStack

import numpy as np

import concourse.bass as bass
from concourse import mybir

F32 = mybir.dt.float32
F32R = mybir.dt.float32r
BF16 = mybir.dt.bfloat16
ALU = mybir.AluOpType
ACT = mybir.ActivationFunctionType
AX_X = mybir.AxisListType.X

B, C, N = 8, 512, 1024
P = 128
HEADS = 8
D = C // HEADS
CT = C // P
NT = N // P
HALF = 512
NH = N // HALF
GROUPS = 32
GC = C // GROUPS
EPS = 1e-5
XT_SLOTS = 4
GRAN = 16
HI, LO = 0, 1
THREE = ((HI, HI), (HI, LO), (LO, HI))


class Arena:

    def __init__(self, tensor, size):
        self.tensor, self.size, self.at = tensor, size, 0

    def take(self, *shape):
        n = int(np.prod(shape))
        assert self.at + n <= self.size, (self.at, n, self.size)
        view = self.tensor[:, self.at:self.at + n]
        self.at += n
        if len(shape) > 1:
            names = "abcdef"[:len(shape)]
            view = view.rearrange(f"p ({' '.join(names)}) -> p {' '.join(names)}",
                                  **dict(zip(names[1:], shape[1:])))
        return view


def f(ap):
    return ap.bitcast(F32)


def build(nc, x, wq_t, wv_t, wk, wo_t, bq0, bv0, bk0, bo0, gamma0, beta0, gamma1, beta1, w1, bqkv1, bproj1, out):
    y_dram = nc.dram_tensor("y_dram", [B, C, N], F32).ap()
    w1_dram = nc.dram_tensor("w1_dram", [GRAN, P, 2, CT, P], F32R).ap()

    x_v = x.rearrange("b (j p) n -> b p j n", p=P)
    y_v = y_dram.rearrange("b (j p) n -> b p j n", p=P)
    out_v = out.rearrange("b (j p) n -> b p j n", p=P)

    def rows(w):
        return w.rearrange("(j p) m -> p j m", p=P)

    def column(v):
        return v.rearrange("(j p) -> p j", p=P)

    with ExitStack() as ctx:
        def sb(name, shape, dt):
            return ctx.enter_context(nc.sbuf_tensor(name, shape, dt))

        def sem(name):
            return ctx.enter_context(nc.semaphore(name))

        R_SIZE, A_SIZE = 152 * 256, 50 * 256
        r_all = sb("r_all", [P, R_SIZE], F32R)
        a_all = sb("a_all", [P, A_SIZE], F32)

        r0, a0 = Arena(r_all, R_SIZE), Arena(a_all, A_SIZE)
        w_q, w_v, w_k, w_o = (r0.take(2, CT, C) for _ in range(4))
        xs = r0.take(2, CT, N)
        xt = r0.take(XT_SLOTS, 2, C)
        gs = us = r0.take(2, CT, C)
        ts = a_s = r0.take(2, CT, C)
        ms = r0.take(2, CT, P)
        gran_s = r0.take(2, CT, P)
        x32 = a0.take(CT, N)
        y32 = a0.take(2, CT, HALF)
        stage32 = a0.take(2, C)
        row2 = a0.take(C)
        bias_rows = a0.take(2, C)
        eye_wide = a0.take(C + C - P)
        gran32 = a0.take(CT, P)
        stats = a0.take(CT, B * NH, 6)
        group_avg = a0.take(P)
        w32 = y32.rearrange("p a j n -> p a (j n)").rearrange("p a (j m) -> p a j m", j=CT)

        r1, a1 = Arena(r_all, R_SIZE), Arena(a_all, A_SIZE)
        w_v1 = r1.take(CT, 2, CT, P)
        w_s = r1.take(2, 2, 2, CT, P)
        xn = r1.take(2, CT, N)
        q_a = r1.take(2, 2, N)
        k_a = r1.take(2, 2, N)
        k_b = r1.take(2, 2, N)
        q_b = r1.take(2, N)
        hid = r1.take(2, CT, N)
        v_t = a1.take(NT, C)
        probs = a1.take(2, 2, N)
        res32 = probs.rearrange("p a h n -> p (a h) n")
        y_half = a1.take(2, HALF)
        y_first = v_t.rearrange("p (j h) n -> p j (h n)", j=CT)
        p_sum = a1.take(2, N)
        o32 = a1.take(N)
        recip = a1.take(HALF)

        SMALL = 724
        small = sb("small", [P, SMALL], F32)
        s = Arena(small, SMALL)
        eye = s.take(P)
        ones64 = s.take(D)
        max2 = s.take(2, NT, NH)
        max_cols = s.take(4, 32)
        mean_var = s.take(CT, B, 2)
        bn_mv = s.take(CT, 2)
        bn_var = s.take(CT)
        root_tmp = s.take(CT * B)
        gn_in = s.take(CT, B)
        gn_mean = s.take(CT, B)
        x1_mean = s.take(CT, B)
        gn_tmp = s.take(CT, B)
        xn_scale, xn_bias = s.take(CT, B), s.take(CT, B)
        bn_scale, bn_bias, res_bias = s.take(CT), s.take(CT), s.take(CT)
        c_sum, c_vec, s_col = s.take(CT), s.take(CT), s.take(CT)
        bo_c, bk_c, g0_c, b0_c, g1_c, b1_c, bp_c = (s.take(CT) for _ in range(7))
        bqkv_c = s.take(3 * CT)
        bk_s = sb("bk_s", [P, CT, 2], F32R)
        s_s = sb("s_s", [P, CT, 2], F32R)
        mask = sb("mask", [64, NT, P], BF16)

        psum = [ctx.enter_context(nc.psum_tensor(f"psum{i}", [P, 2, HALF], F32)) for i in range(4)]

        def bank(i):
            return psum[i // 2][:, i % 2, :]

        w_loaded = [sem("w_loaded0"), sem("w_loaded1")]
        consts_loaded = sem("consts_loaded")
        x_loaded = [sem(f"x_loaded{h}") for h in range(NH)]
        y_stored = [sem(f"y_stored{h}") for h in range(NH)]
        w_hi_done = sem("w_hi_done")
        w_lo_done = sem("w_lo_done")
        consts_ready = sem("consts_ready")
        dve_step = sem("dve_step")
        pool_step = sem("pool_step")
        x_hi_done = sem("x_hi_done")
        x_lo_done = sem("x_lo_done")
        ring_full = sem("ring_full")
        ring_free = sem("ring_free")
        hi_done = sem("hi_done")
        lo_done = sem("lo_done")
        xt_used = sem("xt_used")
        x_summed = sem("x_summed")
        g_full = sem("g_full")
        u_full = sem("u_full")
        u_ready = sem("u_ready")
        m_full = sem("m_full")
        m_split = sem("m_split")
        c_full = sem("c_full")
        c_ready = sem("c_ready")
        y_full = sem("y_full")
        y_ready = sem("y_ready")
        y_counted = sem("y_counted")
        gran_loaded = sem("gran_loaded")
        gran_split = sem("gran_split")
        gran_stored = sem("gran_stored")
        pads_ready = sem("pads_ready")
        gn_moved = sem("gn_moved")
        gn_averaged = sem("gn_averaged")
        norm_ready = sem("norm_ready")
        var_ready = sem("var_ready")
        root_ready = sem("root_ready")
        wv1_loaded = sem("wv1_loaded")
        ws_loaded = [sem("ws_loaded0"), sem("ws_loaded1")]
        y_first_loaded = sem("y_first_loaded")
        y_half_loaded = [sem("y_half_loaded0"), sem("y_half_loaded1")]
        xn_made = sem("xn_made")
        xn_hi_done = sem("xn_hi_done")
        xn_lo_done = sem("xn_lo_done")
        work_full = sem("work_full")
        work_free = sem("work_free")
        qk_hi_done = sem("qk_hi_done")
        k_twice = sem("k_twice")
        max_ready = sem("max_ready")
        q_b_ready = sem("q_b_ready")
        scores_full = sem("scores_full")
        probs_ready = sem("probs_ready")
        pv_done = sem("pv_done")
        sum_step = sem("sum_step")
        o_ready = sem("o_ready")
        o_normed = sem("o_normed")
        hid_hi_done = sem("hid_hi_done")
        hid_lo_done = sem("hid_lo_done")
        res_loaded = sem("res_loaded")
        res_scaled = sem("res_scaled")
        out_stored = [sem("out_stored0"), sem("out_stored1")]

        block = ctx.enter_context(nc.Block())

        T0, U0, A0, RING0 = NT, NT + CT, NT + 2 * CT, NT + 3 * CT
        G_S, T_S, U_S, A_S, SPLITS = NT, NT + CT, NT + 2 * CT, NT + 3 * CT, NT + 4 * CT
        AHEAD = 3

        def ring_bank(t):
            return bank(4 + t % 4)

        PAIRS = CT
        QK, SMAX, SUMS = 2 * NH, 2 * NT * NH, NH
        WORK0 = QK + SMAX + 1 + NT
        WORK = PAIRS * (QK + SMAX + 1 + SUMS) + NT + CT * NH
        assert WORK % 2 == 0
        NEXT = QK + SMAX + 1

        def qk_used(b, p):
            return b * WORK + (WORK0 + p * (NEXT + SUMS) + QK)

        def sums_used(b, p, last):
            if p == 0:
                return b * WORK + (WORK0 - CT * NH - (NT - 5))
            return b * WORK + (WORK0 + p * (NEXT + SUMS) + (0 if last and p == PAIRS - 1 else QK // 2))

        def proj_used(b, t, last):
            return b * WORK + (WORK0 + WORK - CT * NH - (NEXT + NT if last else 0) + t)

        ROWS = (0, 0, 3, 6, 6, 6, 6, 5)
        PLACE0 = (0, 0, 4, 0, 0, 0, 0, 0)
        assert len(ROWS) == NT and sum(ROWS) == SMAX
        NORM_ROW = (-1, -1, 4, 7, 11, 14, 18, 22)
        LO_ROW = (0, 1, 6, 9, 13, 16, 20, 24)

        SCALE = 1.0 / float(np.sqrt(D))

        ONE = 1

        class Tally:

            def __init__(self):
                self.base, self.n, self.started = 0, 0, False

            def start(self, b):
                self.base, self.n, self.started = b * WORK, WORK0, True

            def next(self):
                self.n += 1
                return self.base + self.n, bank(6 + self.n % 2)

            def upto(self, n=0):
                return self.base + self.n - n

        @block.sync
        def _(sp):
            for h in range(NH):
                sp.dma_start(x32[:, :, h * HALF:(h + 1) * HALF], x_v[0, :, :, h * HALF:(h + 1) * HALF]).then_inc(x_loaded[h], 16)
            weights = (wv_t, wq_t, wo_t, wk)
            for w in range(2):
                sp.dma_start(w32[:, w], rows(weights[w])).then_inc(w_loaded[w], 16)
            for i, (to, of) in enumerate((
                    (bias_rows[:, 0], bq0.rearrange("(a n) -> a n", a=1).to_broadcast([P, C])),
                    (bias_rows[:, 1], bv0.rearrange("(a n) -> a n", a=1).to_broadcast([P, C])))):
                sp.dma_start(to, of).then_inc(consts_loaded, 16)
            for to, of in ((bo_c, bo0), (bk_c, bk0), (g0_c, gamma0), (b0_c, beta0), (g1_c, gamma1), (b1_c, beta1),
                           (bp_c, bproj1), (bqkv_c, bqkv1)):
                with nc.allow_non_contiguous_dma(reason="a bias column, 2 KB in all"):
                    sp.dma_start(to, column(of)).then_inc(consts_loaded, 16)
            for w in range(2, 4):
                sp.wait_ge(w_lo_done, w - 1)
                sp.dma_start(w32[:, w % 2], rows(weights[w])).then_inc(w_loaded[w % 2], 16)
            def store_y(b):
                for h in range(NH):
                    sp.wait_ge(y_ready, b * NH * CT + (h + 1) * CT)
                    sp.dma_start(y_v[b, :, :, h * HALF:(h + 1) * HALF], y32[:, h]).then_inc(y_stored[h], 16)

            def x_free(b):
                sp.wait_ge(x_lo_done, (b + 1) * CT)
                sp.wait_ge(ring_full, b * RING0 + NT)

            with sp.Fori(0, B - 1) as b:
                x_free(b)
                for h in range(NH):
                    cols = slice(h * HALF, (h + 1) * HALF)
                    sp.dma_start(x32[:, :, cols], x_v[b + 1, :, :, cols]).then_inc(x_loaded[h], 16)
                store_y(b)

            x_free(B - 1)
            for h in range(NH):
                sp.wait_ge(y_stored[h], 16 * (B - 1))
            sp.dma_start(y_first, y_v[0]).then_inc(y_first_loaded, 16)
            sp.wait_ge(m_full, B * CT)
            sp.wait_ge(gran_stored, GRAN * 16)

            def pieces(first, n):
                return f(w1_dram[first:first + n].rearrange("g p a j m -> p g (a j m)"))

            def load_stream(slot, first):
                sp.dma_start(f(w_s[:, slot].rearrange("p g a j m -> p g (a j m)")), pieces(first, 2)).then_inc(ws_loaded[slot], 16)

            def load_y(b, us_):
                for u in us_:
                    if u >= 2:
                        sp.wait_ge(xn_lo_done, b * NH * CT + u - 1)
                    src = y_v[b, :, u // NH, u % NH * HALF:(u % NH + 1) * HALF]
                    sp.dma_start(y_half[:, u % 2], src).then_inc(y_half_loaded[u % 2], 16)

            load_stream(1, 0)
            sp.dma_start(f(w_v1.rearrange("p g a j m -> p g (a j m)")), pieces(3 * CT, CT)).then_inc(wv1_loaded, 16)
            load_stream(0, 2)
            store_y(B - 1)
            for h in range(NH):
                sp.wait_ge(y_stored[h], 16 * B)

            for half in out_stored:
                sp.sem_inc(half, ONE)
            sp.wait_ge(work_full, QK)
            load_stream(1, 4)

            def batch1(b, last):
                sp.wait_ge(work_full, qk_used(b, 0))
                load_stream(0, 6)
                sp.wait_ge(work_full, qk_used(b, 1))
                load_stream(1, 10 if last else 0)
                if not last:
                    load_y(b + 1, range(2))
                if not last:
                    load_y(b + 1, range(2, NH * CT))
                sp.wait_ge(work_full, qk_used(b, 2))
                load_stream(0, 8)
                if not last:
                    sp.wait_ge(work_full, qk_used(b, 3))
                    load_stream(1, 10)
                sp.wait_ge(pv_done, ONE + (b + 1) * PAIRS * NT)
                sp.wait_ge(sum_step, ONE + (b + 1) * PAIRS * 2 * (NT - 1))
                sp.dma_start(res32, y_v[b]).then_inc(res_loaded, 16)
                for o in range(CT):
                    sp.wait_ge(work_free, proj_used(b, (o + 1) * NH, last))
                    sp.dma_start(out_v[b, :, o], res32[:, o]).then_inc(out_stored[o // 2], 16)
                    if not last and o % 2:
                        load_stream(o // 2, 2 + o // 2 * 2)

            with sp.Fori(0, B - 1) as b:
                batch1(b, False)
            batch1(B - 1, True)
            for half in out_stored:
                sp.wait_ge(half, ONE + B * CT // 2 * 16)

        @block.gpsimd
        def _(pool):
            pool.memset(eye_wide, 0.0).then_inc(pool_step, 1)
            pool.memset(eye, 0.0).then_inc(pool_step, 1)
            pool.memset(mask[:, :, :], 0.0).then_inc(pool_step, 1)
            pool.memset(group_avg, 1.0 / GC).then_inc(pool_step, 1)
            pool.memset(ones64, 1.0).then_inc(pool_step, 1)
            pool.memset(f(ms), 0.0).then_inc(pool_step, 1)
            pool.wait_ge(pool_step, 6)
            mid = eye_wide[:, C - P:C]
            pool.affine_select(out=mid, in_=mid, compare_op=ALU.not_equal, fill=1.0, base=0,
                               pattern=[[-1, P]], channel_multiplier=1).then_inc(pool_step, 1)
            pool.wait_ge(pool_step, 7)
            pool.affine_select(out=eye, in_=eye, compare_op=ALU.not_equal, fill=1.0, base=0,
                               pattern=[[-1, P]], channel_multiplier=1).then_inc(pool_step, 1)
            for h in range(2):
                pool.wait_ge(pool_step, 8 + h)
                pool.affine_select(out=mask[32 * h:32 * h + 32, :, :], in_=mask[32 * h:32 * h + 32, :, :],
                                   compare_op=ALU.not_equal, fill=-1.0, base=0,
                                   pattern=[[-1, NT], [0, P]], channel_multiplier=1).then_inc(pool_step, 1)
            blocks = group_avg.rearrange("p (g c) -> p g c", c=GC)
            pool.wait_ge(pool_step, 10)
            pool.affine_select(out=blocks, in_=blocks, compare_op=ALU.is_ge, fill=0.0, base=0,
                               pattern=[[-GC, P // GC], [0, GC]], channel_multiplier=1).then_inc(pool_step, 1)
            pool.wait_ge(pool_step, 11)
            pool.affine_select(out=blocks, in_=blocks, compare_op=ALU.is_ge, fill=0.0, base=GC - 1,
                               pattern=[[GC, P // GC], [0, GC]], channel_multiplier=-1).then_inc(pool_step, 1)
            pool.wait_ge(pool_step, 12)
            pool.sem_inc(consts_ready, 1)
            with pool.Fori(0, GRAN) as g:
                pool.dma_start(gran32, w1[g]).then_inc(gran_loaded, 16)
                pool.wait_ge(gran_loaded, g * 16 + 16)
                pool.tensor_tensor(gran_s[:, HI], gran32, ones64[:, 0:1].unsqueeze(1).to_broadcast([P, CT, P]), ALU.mult).then_inc(gran_split, 1)
                pool.wait_ge(gran_split, g * 2 + 1)
                pool.tensor_tensor(gran_s[:, LO], gran32, f(gran_s[:, HI]), ALU.subtract).then_inc(gran_split, 1)
                pool.wait_ge(gran_split, g * 2 + 2)
                pool.dma_start(w1_dram[g], gran_s).then_inc(gran_stored, 16)
                pool.wait_ge(gran_stored, g * 16 + 16)

            pool.sem_inc(sum_step, ONE)
            pool.wait_ge(y_full, B * NH * CT)
            n = 0
            for h in range(2):
                pad = slice(D - h * D, 2 * D - h * D)
                pick = slice(D - h * D, D - h * D + NT)
                for to, value in ((q_b[pad, h], 0.0), (k_b[pad, 0, h], 0.0), (k_b[pad, 1, h], 0.0),
                                  (k_b[pick, 0, h], 1.0), (k_b[pick, 1, h], 1.0)):
                    if n:
                        pool.wait_ge(pads_ready, n)
                    pool.memset(f(to), value).then_inc(pads_ready, 1)
                    n += 1

            def batch1(b, last):
                for p in range(PAIRS):
                    for i in range(1, NT):
                        for h in range(2):
                            if i == 1 and h == 0:
                                pool.wait_ge(work_full, sums_used(b, p, last))
                            pool.wait_ge(probs_ready, ONE + b * PAIRS * 2 * NT + p * 2 * NT + 2 * i + h + 1)
                            pool.wait_ge(sum_step, ONE + b * PAIRS * 2 * (NT - 1) + p * 2 * (NT - 1) + 2 * (i - 1) + h)
                            pool.tensor_tensor(p_sum[:, h], probs[:, 0, h] if i == 1 else p_sum[:, h],
                                               probs[:, i % 2, h], ALU.add).then_inc(sum_step, 1)

            with pool.Fori(0, B - 1) as b:
                batch1(b, False)
            batch1(B - 1, True)

        @block.scalar
        def _(act):
            def hi(to, of):
                act.activation(to, of, ACT.Copy).then_inc(hi_done, 1)

            def w_hi(w):
                act.wait_ge(w_loaded[w % 2], 16 * (w // 2 + 1))
                act.activation((w_v, w_q, w_o, w_k)[w][:, HI], w32[:, w % 2], ACT.Copy).then_inc(w_hi_done, 1)

            def xt_hi(b, n, first=False):
                act.wait_ge(ring_full, b * RING0 + n + 1)
                if not first or n >= XT_SLOTS:
                    act.wait_ge(xt_used, b * NT + n - XT_SLOTS + 1)
                hi(xt[:, n % XT_SLOTS, HI], ring_bank(n))

            def batch(b, first, last):
                for n in range(0 if first else AHEAD, NT):
                    xt_hi(b, n, first)
                    if 3 <= n < 3 + CT:
                        if n == 3:
                            for h in range(NH):
                                act.wait_ge(x_loaded[h], b * 16 + 16)
                            if not first:
                                act.wait_ge(y_full, b * NH * CT)
                        act.activation(xs[:, HI, n - 3], x32[:, n - 3], ACT.Copy).then_inc(x_hi_done, 1)
                    if first and n in (3, 5):
                        w_hi(n // 2 - 1)
                for g in range(CT):
                    act.wait_ge(g_full, b * CT + g + 1)
                    hi(gs[:, HI, g], bank(g))
                if first:
                    w_hi(2)
                for o in range(CT):
                    act.wait_ge(ring_free, b * 2 * CT + o + 1)
                    hi(ts[:, HI, o], stage32[:, o % 2])
                if first:
                    w_hi(3)
                for g in range(CT):
                    act.wait_ge(ring_full, b * RING0 + U0 + g + 1)
                    hi(us[:, HI, g], ring_bank(U0 + g))
                for g in range(CT):
                    act.wait_ge(ring_free, b * 2 * CT + CT + g + 1)
                    hi(a_s[:, HI, g], stage32[:, g % 2])
                act.wait_ge(c_ready, b + 1)
                for h in range(NH):
                    act.wait_ge(y_stored[h], b * 16)
                    act.wait_ge(y_counted, b * NH * CT)
                    for o in range(CT):
                        act.wait_ge(y_full, b * NH * CT + h * CT + o + 1)
                        act.activation(y32[:, h, o], bank(o), ACT.Identity, bias=c_vec[:, o:o + 1]).then_inc(y_ready, 1)
                    if h == 0 and not last:
                        for n in range(AHEAD):
                            xt_hi(b + 1, n)

            batch(0, True, False)
            with act.Fori(1, B - 1) as b:
                batch(b, False, False)
            batch(B - 1, False, True)

            work = Tally()

            def norm_half(b, u, first=False):
                j, cols = u // NH, slice(u % NH * HALF, (u % NH + 1) * HALF)
                act.wait_ge(xn_made, b * NH * CT + u + 1)
                of = y_first[:, j, cols] if first else y_half[:, u % 2]
                act.activation(xn[:, HI, j, cols], of, ACT.Copy).then_inc(xn_hi_done, 1)

            def qk_hi(b, pair, par, i, count):
                n, ps = work.next()
                act.wait_ge(work_full, n)
                of_k, cols = i // 2, slice(i % 2 * HALF, (i % 2 + 1) * HALF)
                bias = bqkv_c[:, of_k * CT + pair:of_k * CT + pair + 1]
                to = (q_a, k_a)[of_k]
                for h in range(2):
                    rows_ = slice(h * D, h * D + D)
                    act.activation(to[rows_, par, h, cols], ps[rows_, :], ACT.Identity, bias=bias[rows_]).then_inc(qk_hi_done, 1)
                if of_k:
                    act.wait_ge(qk_hi_done, 2 * (count + i + 1))
                    for h in range(2):
                        rows_, others = slice(h * D, h * D + D), slice(D - h * D, 2 * D - h * D)
                        act.activation(k_a[others, par, h, cols], f(k_a[rows_, par, h, cols]), ACT.Copy).then_inc(k_twice, 1)

            def q_b_hi(par):
                for h in range(2):
                    rows_ = slice(h * D, h * D + D)
                    act.activation(q_b[rows_, h], f(q_a[rows_, par, h]), ACT.Copy).then_inc(q_b_ready, 1)

            def hid_hi(b, pair, h):
                cols = slice(h * HALF, (h + 1) * HALF)
                act.wait_ge(o_normed, ONE + b * PAIRS * NH + pair * NH + h + 1)
                act.activation(hid[:, HI, pair, cols], o32[:, cols], ACT.Identity,
                               bias=bqkv_c[:, 2 * CT + pair:2 * CT + pair + 1]).then_inc(hid_hi_done, 1)

            for i, (v, root) in enumerate(((bn_var, bn_scale), (gn_in, gn_tmp))):
                act.wait_ge(var_ready, i + 1)
                act.activation(root, v, ACT.Sqrt).then_inc(root_ready, 1)
            act.sem_inc(probs_ready, ONE)
            act.sem_inc(o_ready, ONE)
            act.wait_ge(norm_ready, 1)
            for u in range(NH * CT):
                norm_half(0, u, True)
            for i in range(QK):
                qk_hi(0, 0, 0, i, 0)
            q_b_hi(0)

            def batch1(b, last):
                work.start(b)
                for p in range(PAIRS):
                    more = p < PAIRS - 1 or not last
                    par, pairs = (p + 1) % 2, b * PAIRS + p

                    def next_qk(i):
                        if more:
                            qk_hi(b, (p + 1) % PAIRS, par, i, (pairs + 1) * QK)

                    next_qk(0)
                    for i in range(NT):
                        for h in range(2):
                            act.wait_ge(scores_full, pairs * 2 * NT + 2 * i + h + 1)
                            if h == 0 and i >= 2:
                                act.wait_ge(pv_done, ONE + pairs * NT + i - 1)
                            if i >= 2:
                                act.wait_ge(sum_step, ONE + pairs * 2 * (NT - 1) + 2 * (max(i - 2, 1) - 1) + h + 1)
                            elif p == 0 and h == 0:
                                if i == 0:
                                    act.wait_ge(sum_step, ONE + pairs * 2 * (NT - 1))
                                    act.wait_ge(pv_done, ONE + pairs * NT)
                                act.wait_ge(out_stored[i], ONE + b * CT // 2 * 16)
                            elif p:
                                act.wait_ge(sum_step, ONE + pairs * 2 * (NT - 1) - 2 * (1 - i) - 1 + h)
                            act.activation(probs[:, i % 2, h], psum[h][:, :, :].rearrange("p a n -> p (a n)"), ACT.Exp,
                                           scale=SCALE).then_inc(probs_ready, 1)
                        if p and i < NH:
                            work.next()
                        if i == 0:
                            next_qk(1)
                        if i == 1:
                            next_qk(2)
                            if p:
                                hid_hi(b, p - 1, 0)
                            next_qk(3)
                            if p:
                                hid_hi(b, p - 1, 1)
                        if more:
                            for _ in range(ROWS[i]):
                                work.next()
                        if p == 2 and not last:
                            if i == 1:
                                act.wait_ge(work_full, qk_used(b, 2))
                                for u in range(2):
                                    norm_half(b + 1, u)
                            for u in range(NH * CT):
                                if sum(ROWS[:i]) <= NORM_ROW[u] < sum(ROWS[:i + 1]):
                                    norm_half(b + 1, u)
                    if more:
                        work.next()
                        q_b_hi(par)
                    act.wait_ge(hid_lo_done, ONE + pairs * NH)
                    act.wait_ge(pv_done, ONE + (pairs + 1) * NT)
                    act.activation(o32, psum[2][:, :, :].rearrange("p a n -> p (a n)"), ACT.Copy).then_inc(o_ready, 1)
                for h in range(NH):
                    hid_hi(b, PAIRS - 1, h)
                act.wait_ge(res_loaded, (b + 1) * 16)
                for o in range(CT):
                    act.activation(res32[:, o], res32[:, o], ACT.Identity, scale=bn_scale[:, o:o + 1],
                                   bias=res_bias[:, o:o + 1]).then_inc(res_scaled, 1)

            with act.Fori(0, B - 1) as b:
                batch1(b, False)
            batch1(B - 1, True)

        @block.vector
        def _(dve):
            def split_w(w):
                to = (w_v, w_q, w_o, w_k)[w]
                dve.wait_ge(w_hi_done, w + 1)
                dve.tensor_tensor(to[:, LO], w32[:, w % 2], f(to[:, HI]), ALU.subtract).then_inc(w_lo_done, 1)

            dve.wait_ge(consts_ready, 1)
            FIRST, STEPS = 2, 2 * CT + 1

            def lo(to, of, hi_part):
                dve.tensor_tensor(to, of, f(hi_part), ALU.subtract).then_inc(lo_done, 1)

            def xt_lo(b, n):
                dve.wait_ge(hi_done, b * SPLITS + n + 1)
                to = xt[:, n % XT_SLOTS]
                lo(to[:, LO], ring_bank(n), to[:, HI])

            def batch(b, first, last):
                for n in range(0 if first else AHEAD, NT):
                    xt_lo(b, n)
                    j = n - 3
                    if 0 <= j < CT:
                        if j == 0:
                            dve.wait_ge(x_summed, b * (CT + 2))
                            for h in range(NH):
                                dve.wait_ge(x_loaded[h], b * 16 + 16)
                        dve.reduce_sum(s_col[:, j:j + 1], x32[:, j], AX_X).then_inc(x_summed, 1)
                        dve.wait_ge(x_hi_done, b * CT + j + 1)
                        dve.tensor_tensor(xs[:, LO, j], x32[:, j], f(xs[:, HI, j]), ALU.subtract).then_inc(x_lo_done, 1)
                    if first and n in (3, 5):
                        split_w(n // 2 - 1)
                dve.wait_ge(x_summed, b * (CT + 2) + CT)
                dve.tensor_copy(s_s[:, :, HI], s_col).then_inc(x_summed, 1)
                dve.wait_ge(x_summed, b * (CT + 2) + CT + 1)
                dve.tensor_tensor(s_s[:, :, LO], s_col, f(s_s[:, :, HI]), ALU.subtract).then_inc(x_summed, 1)
                for g in range(CT):
                    dve.wait_ge(hi_done, b * SPLITS + G_S + g + 1)
                    lo(gs[:, LO, g], bank(g), gs[:, HI, g])
                if first:
                    split_w(2)
                    dve.wait_ge(consts_loaded, 10 * 16)
                    dve.tensor_copy(bk_s[:, :, HI], bk_c).then_inc(dve_step, 1)
                    dve.wait_ge(dve_step, 1)
                    dve.tensor_tensor(bk_s[:, :, LO], bk_c, f(bk_s[:, :, HI]), ALU.subtract).then_inc(dve_step, 1)

                dve.wait_ge(u_full, 2 * b + 1)
                dve.scalar_tensor_tensor(out=row2[0:2], in0=bias_rows[0:2, 1], scalar=N / 2, in1=bank(3)[0:2, :],
                                         op0=ALU.mult, op1=ALU.add).then_inc(u_ready, 1)

                def t_lo(o):
                    dve.wait_ge(hi_done, b * SPLITS + T_S + o + 1)
                    lo(ts[:, LO, o], stage32[:, o % 2], ts[:, HI, o])

                for o in range(CT):
                    dve.wait_ge(ring_full, b * RING0 + T0 + o + 1)
                    if not first or o >= 2:
                        dve.wait_ge(lo_done, b * SPLITS + (T_S + o - 1 if o >= 2 else 0))
                    dve.scalar_tensor_tensor(out=stage32[:, o % 2], in0=bias_rows[:, 1], scalar=s_col[:, o:o + 1],
                                             in1=ring_bank(T0 + o), op0=ALU.mult, op1=ALU.add).then_inc(ring_free, 1)
                    if o:
                        t_lo(o - 1)
                t_lo(CT - 1)
                if first:
                    split_w(3)
                for g in range(CT):
                    dve.wait_ge(m_full, b * CT + g + 1)
                    if g == 0:
                        dve.wait_ge(m_split, b * 2 * CT)
                    for e in range(2):
                        part = slice(e * D, e * D + D)
                        of = bank(g)[part, g % 2 * P + e * D:g % 2 * P + e * D + D]
                        dve.tensor_copy(ms[part, HI, g, part], of).then_inc(dve_step, 1)
                    dve.wait_ge(dve_step, b * STEPS + FIRST + 2 * g + 2)
                    for e in range(2):
                        part = slice(e * D, e * D + D)
                        of = bank(g)[part, g % 2 * P + e * D:g % 2 * P + e * D + D]
                        dve.tensor_tensor(ms[part, LO, g, part], of, f(ms[part, HI, g, part]),
                                          ALU.subtract).then_inc(m_split, 1)
                for g in range(CT):
                    dve.wait_ge(hi_done, b * SPLITS + U_S + g + 1)
                    lo(us[:, LO, g], ring_bank(U0 + g), us[:, HI, g])
                dve.wait_ge(u_full, 2 * b + 2)
                dve.wait_ge(u_ready, 2 * b + 1)
                dve.tensor_copy(row2[0:2], bank(3)[0:2, :]).then_inc(u_ready, 1)

                def a_lo(g):
                    dve.wait_ge(hi_done, b * SPLITS + A_S + g + 1)
                    lo(a_s[:, LO, g], stage32[:, g % 2], a_s[:, HI, g])

                for g in range(CT):
                    dve.wait_ge(ring_full, b * RING0 + A0 + g + 1)
                    dve.wait_ge(lo_done, b * SPLITS + A_S + max(0, g - 1))
                    dve.tensor_tensor(stage32[:, g % 2], ring_bank(A0 + g), eye_wide[:, C - P - g * P:2 * C - P - g * P],
                                      ALU.add).then_inc(ring_free, 1)
                    if g:
                        a_lo(g - 1)
                a_lo(CT - 1)
                dve.wait_ge(c_full, b + 1)
                dve.wait_ge(c_ready, b)
                dve.tensor_copy(c_sum, bank(2)[:, 0:2 * CT].rearrange("p (o t) -> p o t", t=2)[:, :, 0]).then_inc(dve_step, 1)
                dve.wait_ge(dve_step, b * STEPS + FIRST + STEPS)
                dve.wait_ge(y_ready, b * NH * CT)
                dve.tensor_tensor(c_vec, c_sum, bo_c, ALU.add).then_inc(c_ready, 1)
                for h in range(NH):
                    for o in range(CT):
                        dve.wait_ge(y_ready, b * NH * CT + h * CT + o + 1)
                        if first or last:
                            to = stats[:, o, b * NH + h, :]
                        else:
                            to = stats[:, o, bass.ds(b * NH + h, 1), :].rearrange("p a k -> p (a k)")
                        dve.bn_stats(to, y32[:, h, o]).then_inc(y_counted, 1)
                    if h == 0 and not last:
                        for n in range(AHEAD):
                            xt_lo(b + 1, n)

            batch(0, True, False)
            with dve.Fori(1, B - 1) as b:
                batch(b, False, False)
            batch(B - 1, False, True)

            steps = FIRST + B * STEPS

            def then(ins):
                nonlocal steps
                steps += 1
                ins.then_inc(dve_step, 1)
                dve.wait_ge(dve_step, steps)

            def invert(root, v, tmp):
                then(dve.reciprocal(root, root))
                then(dve.tensor_tensor(tmp, root, root, ALU.mult))
                then(dve.tensor_tensor(tmp, tmp, v, ALU.mult))
                then(dve.tensor_scalar(tmp, tmp, -0.5, 1.5, ALU.mult, ALU.add))
                then(dve.tensor_tensor(root, root, tmp, ALU.mult))

            def wide(v):
                return v.unsqueeze(2).to_broadcast([P, CT, B])

            dve.wait_ge(y_counted, B * NH * CT)
            for j in range(CT):
                dve.bn_aggr(bn_mv[:, j], stats[:, j].rearrange("p a k -> p (a k)")).then_inc(dve_step, 1)
                for b in range(B):
                    dve.bn_aggr(mean_var[:, j, b], stats[:, j, b * NH:(b + 1) * NH].rearrange("p a k -> p (a k)")).then_inc(dve_step, 1)
            steps += CT * (B + 1)
            dve.wait_ge(dve_step, steps)
            dve.tensor_scalar(bn_var, bn_mv[:, :, 1], EPS, None, ALU.add).then_inc(var_ready, 1)
            dve.wait_ge(root_ready, 1)
            invert(bn_scale, bn_var, root_tmp[:, 0:CT])
            then(dve.tensor_tensor(bn_scale, bn_scale, g0_c, ALU.mult))
            then(dve.tensor_tensor(bn_bias, bn_mv[:, :, 0], bn_scale, ALU.mult))
            then(dve.tensor_tensor(bn_bias, b0_c, bn_bias, ALU.subtract))
            then(dve.tensor_tensor(res_bias, bn_bias, bp_c, ALU.add))
            then(dve.tensor_tensor(x1_mean, mean_var[:, :, :, 0], wide(bn_scale), ALU.mult))
            dve.tensor_tensor(x1_mean, x1_mean, wide(bn_bias), ALU.add).then_inc(gn_moved, 1)
            dve.wait_ge(gn_moved, 1)
            dve.wait_ge(gn_averaged, 1)
            then(dve.tensor_copy(gn_mean, bank(6)[:, 0:CT * B].rearrange("p (j b) -> p j b", b=B)))
            then(dve.tensor_tensor(gn_tmp, x1_mean, gn_mean, ALU.subtract))
            then(dve.tensor_tensor(gn_tmp, gn_tmp, gn_tmp, ALU.mult))
            then(dve.tensor_tensor(gn_in, mean_var[:, :, :, 1], wide(bn_scale), ALU.mult))
            then(dve.tensor_tensor(gn_in, gn_in, wide(bn_scale), ALU.mult))
            dve.tensor_tensor(gn_in, gn_in, gn_tmp, ALU.add).then_inc(gn_moved, 1)
            dve.wait_ge(gn_averaged, 2)
            dve.tensor_scalar(gn_in, bank(7)[:, 0:CT * B].rearrange("p (j b) -> p j b", b=B), EPS, None, ALU.add).then_inc(var_ready, 1)
            dve.wait_ge(root_ready, 2)
            invert(gn_tmp, gn_in, root_tmp.rearrange("p (j b) -> p j b", b=B))
            then(dve.tensor_tensor(gn_tmp, gn_tmp, wide(g1_c), ALU.mult))
            then(dve.tensor_tensor(xn_scale, gn_tmp, wide(bn_scale), ALU.mult))
            then(dve.tensor_tensor(xn_bias, wide(bn_bias), gn_mean, ALU.subtract))
            then(dve.tensor_tensor(xn_bias, xn_bias, gn_tmp, ALU.mult))
            then(dve.memset(max_cols, 0.0))
            dve.tensor_tensor(xn_bias, xn_bias, wide(b1_c), ALU.add).then_inc(norm_ready, 1)

            work = Tally()

            def norm(b, u):
                dve.wait_ge(y_half_loaded[u % 2], b * (NH * CT // 2 * 16) - NH * CT // 2 * 16 + (u // 2 + 1) * 16)
                at = [v[:, u // NH, bass.ds(b, 1)] for v in (xn_scale, xn_bias)]
                dve.tensor_scalar(y_half[:, u % 2], y_half[:, u % 2], at[0], at[1], ALU.mult, ALU.add).then_inc(xn_made, 1)

            def norm_lo(b, u):
                j, cols = u // NH, slice(u % NH * HALF, (u % NH + 1) * HALF)
                dve.wait_ge(xn_hi_done, b * NH * CT + u + 1)
                dve.tensor_tensor(xn[:, LO, j, cols], y_half[:, u % 2], f(xn[:, HI, j, cols]), ALU.subtract).then_inc(xn_lo_done, 1)

            def qk_lo(pair, par, i, count):
                n, ps = work.next()
                dve.wait_ge(qk_hi_done, 2 * (count + i + 1))
                of_k, cols = i // 2, slice(i % 2 * HALF, (i % 2 + 1) * HALF)
                bias = bqkv_c[:, of_k * CT + pair:of_k * CT + pair + 1]
                for h in range(2):
                    rows_, others = slice(h * D, h * D + D), slice(D - h * D, 2 * D - h * D)
                    to = k_b[rows_, par, h, cols] if of_k else q_a[others, par, h, cols]
                    ins = dve.scalar_tensor_tensor(out=to, in0=ps[rows_, :], scalar=bias[rows_],
                                                   in1=f((q_a, k_a)[of_k][rows_, par, h, cols]),
                                                   op0=ALU.add, op1=ALU.subtract)
                ins.then_inc(work_free, 1)

            def max_tile(t):
                n, ps = work.next()
                h, tile, half = t // (NT * NH), t // NH % NT, t % NH
                dve.wait_ge(work_full, n)
                dve.reduce_max(max2[:, h, tile, half:half + 1], ps, AX_X).then_inc(work_free, 1)

            def max_join():
                dve.wait_ge(work_free, work.upto())
                dve.tensor_tensor(max_cols[:, 0:2, 0:NT], max2[:, :, :, 0], max2[:, :, :, 1], ALU.max).then_inc(max_ready, 1)

            def max_rows(pairs):
                n, ps = work.next()
                dve.wait_ge(work_full, n)
                dve.wait_ge(scores_full, pairs * 2 * NT)
                for h in range(2):
                    of = ps[32 * h:32 * h + NT, 0:P].unsqueeze(1).to_broadcast([NT, NT, P])
                    to = q_b[D - h * D:D - h * D + NT, h].rearrange("p (j t) -> p j t", j=NT)
                    ins = dve.tensor_tensor(to, of, mask[32 * h:32 * h + NT, :, :], ALU.mult)
                ins.then_inc(work_free, 1)

            def v_tile(b, i):
                n, ps = work.next()
                dve.wait_ge(work_full, n)
                if i == 0:
                    dve.wait_ge(pv_done, ONE + b * PAIRS * NT)
                dve.tensor_copy(v_t[:, i], ps).then_inc(work_free, 1)

            def normalise(b, pair, h):
                n, ps = work.next()
                cols, halves = slice(h * HALF, (h + 1) * HALF), b * PAIRS * NH + pair * NH + h
                dve.wait_ge(work_full, n)
                dve.wait_ge(o_normed, ONE + halves)
                dve.reciprocal(recip, ps).then_inc(work_free, 1)
                if h == 0:
                    dve.wait_ge(o_ready, ONE + b * PAIRS + pair + 1)
                dve.wait_ge(work_free, n)
                dve.tensor_tensor(o32[:, cols], o32[:, cols], recip, ALU.mult).then_inc(o_normed, 1)

            def hid_lo(b, pair, h):
                cols = slice(h * HALF, (h + 1) * HALF)
                dve.wait_ge(hid_hi_done, b * PAIRS * NH + pair * NH + h + 1)
                dve.scalar_tensor_tensor(out=hid[:, LO, pair, cols], in0=o32[:, cols],
                                         scalar=bqkv_c[:, 2 * CT + pair:2 * CT + pair + 1],
                                         in1=f(hid[:, HI, pair, cols]), op0=ALU.add, op1=ALU.subtract).then_inc(hid_lo_done, 1)

            dve.sem_inc(hid_lo_done, ONE)
            dve.sem_inc(o_normed, ONE)
            dve.wait_ge(pads_ready, 10)
            dve.wait_ge(norm_ready, 1)
            dve.wait_ge(y_first_loaded, 16)
            for u in range(NH * CT + 1):
                if u < NH * CT:
                    j, cols = u // NH, slice(u % NH * HALF, (u % NH + 1) * HALF)
                    dve.tensor_scalar(y_first[:, j, cols], y_first[:, j, cols], xn_scale[:, j, 0:1], xn_bias[:, j, 0:1],
                                      ALU.mult, ALU.add).then_inc(xn_made, 1)
                if u:
                    j, cols = (u - 1) // NH, slice((u - 1) % NH * HALF, ((u - 1) % NH + 1) * HALF)
                    dve.wait_ge(xn_hi_done, u)
                    dve.tensor_tensor(xn[:, LO, j, cols], y_first[:, j, cols], f(xn[:, HI, j, cols]), ALU.subtract).then_inc(xn_lo_done, 1)
            for i in range(QK):
                qk_lo(0, 0, i, 0)
            for t in range(SMAX):
                max_tile(t)
            max_join()
            max_rows(0)
            for i in range(NT):
                v_tile(0, i)

            def batch1(b, last):
                work.start(b)
                for p in range(PAIRS):
                    more = p < PAIRS - 1 or not last
                    par, pairs = (p + 1) % 2, b * PAIRS + p

                    def next_qk(i):
                        if more:
                            qk_lo((p + 1) % PAIRS, par, i, (pairs + 1) * QK)

                    next_qk(0)
                    if p:
                        normalise(b, p - 1, 0)
                    next_qk(1)
                    if p:
                        normalise(b, p - 1, 1)
                    next_qk(2)
                    if p:
                        hid_lo(b, p - 1, 0)
                    if p == 2 and not last:
                        for u in range(2):
                            norm(b + 1, u)
                    next_qk(3)
                    if p:
                        hid_lo(b, p - 1, 1)
                    if more:
                        dve.wait_ge(max_ready, pairs + 1)
                        for t in range(SMAX):
                            if p == 2 and not last:
                                for u in range(NH * CT):
                                    if NORM_ROW[u] == t:
                                        norm(b + 1, u)
                                for u in range(NH * CT):
                                    if LO_ROW[u] == t:
                                        norm_lo(b + 1, u)
                            max_tile(t)
                        max_join()
                        max_rows(pairs + 1)
                for i in range(NT):
                    if not last:
                        v_tile(b + 1, i)
                    if i in (2, 4):
                        normalise(b, PAIRS - 1, i // 2 - 1)
                    if i in (5, 6):
                        hid_lo(b, PAIRS - 1, i - 5)
                for t in range(CT * NH):
                    n, ps = work.next()
                    o, cols = t // NH, slice(t % NH * HALF, (t % NH + 1) * HALF)
                    dve.wait_ge(work_full, n)
                    dve.wait_ge(res_scaled, b * CT + o + 1)
                    dve.tensor_tensor(res32[:, o, cols], ps, res32[:, o, cols], ALU.add).then_inc(work_free, 1)

            with dve.Fori(0, B - 1) as b:
                batch1(b, False)
            batch1(B - 1, True)

        @block.tensor
        def _(pe):
            def product(to, pairs):
                for i, (w, m) in enumerate(pairs):
                    last = pe.matmul(to, w, m, start=(i == 0), stop=(i == len(pairs) - 1))
                return last

            def transpose_x(b, n, first=False):
                if n % (NT // NH) == 0:
                    pe.wait_ge(x_loaded[n // (NT // NH)], b * 16 + 16)
                if n >= 4 or not first:
                    pe.wait_ge(lo_done, b * SPLITS + n - 3)
                for j in range(CT):
                    last = pe.transpose(ring_bank(n)[:, j * P:(j + 1) * P], x32[:, j, n * P:(n + 1) * P], eye)
                last.then_inc(ring_full, 1)

            def four_tiles(to, split0, bank_free, stationary, moving, done):
                def step(o, j):
                    for i, (w, m) in enumerate(THREE):
                        last = pe.matmul(to(o), stationary(w, j, o), moving(m, j), start=(j == 0 and i == 0),
                                         stop=(j == CT - 1 and i == 2))
                    return last

                for j in range(2):
                    pe.wait_ge(lo_done, split0 + j + 1)
                    for o in range(CT):
                        if j == 0 and bank_free:
                            bank_free(o)
                        step(o, j)
                pe.wait_ge(lo_done, split0 + CT)
                for o in range(CT):
                    step(o, 2)
                    step(o, 3).then_inc(done, 1)

            def batch(b, first, last_batch):
                def gram(n):
                    pe.wait_ge(lo_done, b * SPLITS + n + 1)
                    for g in range(CT):
                        if n == 0 and not first:
                            pe.wait_ge(y_ready, b * NH * CT - CT + g + 1)
                        for i, (w, m) in enumerate(THREE):
                            last = pe.matmul(bank(g), xt[:, n % XT_SLOTS, w, g * P:(g + 1) * P], xt[:, n % XT_SLOTS, m],
                                             start=(n == 0 and i == 0), stop=(n == NT - 1 and i == 2))
                        if n == NT - 1:
                            last.then_inc(g_full, 1)
                        elif g == CT - 1:
                            last.then_inc(xt_used, 1)

                if first:
                    for n in range(AHEAD):
                        transpose_x(b, n, first)
                for n in range(NT):
                    if n + AHEAD < NT:
                        transpose_x(b, n + AHEAD, first)
                    gram(n)
                    if n == NT - 1:
                        pe.sem_inc(xt_used, 1)
                if first:
                    pe.wait_ge(w_lo_done, 1)
                pe.wait_ge(lo_done, b * SPLITS + NT)
                four_tiles(lambda o: ring_bank(T0 + o), b * SPLITS + G_S, None,
                           lambda w, j, o: gs[:, w, j, o * P:(o + 1) * P], lambda m, j: w_v[:, m, j], ring_full)
                pe.wait_ge(x_summed, (b + 1) * (CT + 2))
                product(bank(3)[0:2, :], [(s_s[:, j], w_v[:, m, j]) for j in range(CT) for m in (HI, LO)]).then_inc(u_full, 1)
                if first:
                    pe.wait_ge(w_lo_done, 2)
                for o in range(CT):
                    pe.wait_ge(lo_done, b * SPLITS + T_S + o + 1)
                    if o == 0:
                        pe.wait_ge(u_ready, 2 * b + 1)
                    for g in range(CT):
                        window = slice(g // 2 * 2 * P, (g // 2 + 1) * 2 * P)
                        for i, (t, w) in enumerate(THREE):
                            pe.matmul(bank(g)[:, 0:2 * P], ts[:, t, o, g * P:(g + 1) * P], w_q[:, w, o, window],
                                      start=(o == 0 and i == 0), stop=False)
                        if o == CT - 1:
                            pe.matmul(bank(g)[:, 0:2 * P], row2[0:2, g * P:(g + 1) * P], bias_rows[0:2, 0, window],
                                      start=False, stop=True).then_inc(m_full, 1)
                if first:
                    pe.wait_ge(w_lo_done, 4)
                for g in range(CT):
                    pe.wait_ge(m_split, b * 2 * CT + 2 * g + 2)
                    product(ring_bank(U0 + g), [(ms[:, i, g], w_o[:, k, g]) for i, k in THREE]).then_inc(ring_full, 1)
                for j in range(CT):
                    pe.wait_ge(lo_done, b * SPLITS + U_S + j + 1)
                    for m in (HI, LO):
                        last = pe.matmul(bank(3)[0:2, :], bk_s[:, j], us[:, m, j], start=(j == 0 and m == HI),
                                         stop=(j == CT - 1 and m == LO))
                last.then_inc(u_full, 1)
                four_tiles(lambda o: ring_bank(A0 + o), b * SPLITS + U_S, None,
                           lambda w, j, o: w_k[:, w, j, o * P:(o + 1) * P], lambda m, j: us[:, m, j], ring_full)
                pe.wait_ge(u_ready, 2 * b + 2)
                for o in range(CT):
                    last = pe.matmul(bank(2)[:, 2 * o:2 * o + 2], row2[0:2, o * P:(o + 1) * P], ones64[0:2, 0:2],
                                     start=True, stop=True)
                last.then_inc(c_full, 1)

                def c_read(o):
                    if o == 2:
                        pe.wait_ge(c_ready, b + 1)

                four_tiles(bank, b * SPLITS + A_S, c_read, lambda w, j, o: a_s[:, w, j, o * P:(o + 1) * P],
                           lambda m, j: xs[:, m, j, 0:HALF], y_full)
                if not last_batch:
                    for n in range(AHEAD):
                        transpose_x(b + 1, n)
                for o in range(CT):
                    pe.wait_ge(y_ready, b * NH * CT + o + 1)
                    product(bank(o), [(a_s[:, w, j, o * P:(o + 1) * P], xs[:, m, j, HALF:N])
                                      for j in range(CT) for w, m in THREE]).then_inc(y_full, 1)

            pe.wait_ge(consts_ready, 1)
            batch(0, True, False)
            with pe.Fori(1, B - 1) as b:
                batch(b, False, False)
            batch(B - 1, False, True)

            for i, of in enumerate((x1_mean, gn_in)):
                pe.wait_ge(gn_moved, i + 1)
                pe.matmul(bank(6 + i)[:, 0:CT * B], group_avg, of.rearrange("p j b -> p (j b)"),
                          start=True, stop=True).then_inc(gn_averaged, 1)
            work = Tally()

            def next_tile():
                n, ps = work.next()
                if work.started or work.n > 2:
                    pe.wait_ge(work_free, n - 2)
                return ps

            def qk_tile(slot, i):
                piece, cols = i // 2, slice(i % 2 * HALF, (i % 2 + 1) * HALF)
                product(next_tile(), [(w_s[:, slot, piece, w, j], xn[:, m, j, cols])
                                      for j in range(CT) for w, m in THREE]).then_inc(work_full, 1)

            def max_tile(par, t):
                h, tile, half = t // (NT * NH), t // NH % NT, t % NH
                pe.matmul(next_tile(), q_a[:, par, h, tile * P:(tile + 1) * P],
                          k_a[:, par, h, half * HALF:(half + 1) * HALF], start=True, stop=True).then_inc(work_full, 1)

            def max_turn(pairs):
                pe.wait_ge(max_ready, pairs + 1)
                pe.transpose(next_tile()[:, 0:P], max_cols.rearrange("p h t -> p (h t)"), eye).then_inc(work_full, 1)

            def v_tile(i):
                product(next_tile(), [(xn[:, m, j, i * P:(i + 1) * P], w_v1[:, :, w, j])
                                      for j in range(CT) for w, m in THREE]).then_inc(work_full, 1)

            def scores(pairs, par, i, between):
                for h in range(2):
                    pe.wait_ge(probs_ready, ONE + pairs * 2 * NT + 2 * max(i - 1, 0) + (h + 1 if i else 0))
                    keys = slice(i * P, (i + 1) * P)
                    for first, (k, q) in ((True, (k_a[:, par, h, keys], q_a[:, par, h])), (False, (k_b[:, par, h, keys], q_b[:, h]))):
                        for half in range(NH):
                            last = pe.matmul(psum[h][:, half], k, q[:, half * HALF:(half + 1) * HALF], start=first, stop=not first)
                        if not first:
                            last.then_inc(scores_full, 1)
                        between(2 * h + (not first))

            def weigh(b, p, i, between):
                pairs = b * PAIRS + p
                pe.wait_ge(probs_ready, ONE + pairs * 2 * NT + 2 * i + 2)
                if i == 0:
                    pe.wait_ge(o_ready, ONE + pairs)
                for half in range(NH):
                    for h in range(2):
                        head = slice((2 * p + h) * D, (2 * p + h + 1) * D)
                        last = pe.matmul(psum[2][h * D:(h + 1) * D, half], v_t[:, i, head],
                                         probs[:, i % 2, h, half * HALF:(half + 1) * HALF], start=(i == 0), stop=(i == NT - 1))
                    if half == NH - 1:
                        last.then_inc(pv_done, 1)
                    between(4 + half)

            def sums(pairs, half):
                ps = next_tile()
                pe.wait_ge(sum_step, ONE + (pairs + 1) * 2 * (NT - 1))
                for h in range(2):
                    last = pe.matmul(ps[h * D:(h + 1) * D, :], ones64, p_sum[:, h, half * HALF:(half + 1) * HALF],
                                     start=True, stop=True)
                last.then_inc(work_full, 1)

            pe.sem_inc(pv_done, ONE)
            pe.wait_ge(xn_lo_done, NH * CT)
            pe.wait_ge(ws_loaded[1], 16)
            for i in range(QK):
                qk_tile(1, i)
            pe.wait_ge(k_twice, QK)
            pe.wait_ge(work_free, QK)
            for t in range(SMAX):
                max_tile(0, t)
            max_turn(0)
            pe.wait_ge(wv1_loaded, 16)
            for i in range(NT):
                v_tile(i)
            pe.wait_ge(work_free, WORK0)

            def batch1(b, last):
                work.start(b)
                loads = b * ((PAIRS + 2) // 2)
                for p in range(PAIRS):
                    more = p < PAIRS - 1 or not last
                    par, pairs = p % 2, b * PAIRS + p
                    def next_qk(i):
                        if more:
                            if i == 0:
                                slot = p % 2
                                pe.wait_ge(ws_loaded[slot], (loads + p // 2 + 1 + slot) * 16)
                                if p == PAIRS - 1:
                                    pe.wait_ge(xn_lo_done, (b + 2) * NH * CT)
                            qk_tile(p % 2, i)

                    next_qk(0)
                    for i in range(NT):
                        def next_row(slot):
                            if more and PLACE0[i] <= slot < PLACE0[i] + ROWS[i]:
                                if i == 2 and slot == PLACE0[i]:
                                    pe.wait_ge(work_free, work.upto())
                                    pe.wait_ge(k_twice, (pairs + 2) * QK)
                                max_tile(1 - par, sum(ROWS[:i]) + slot - PLACE0[i])

                        if i == 0:
                            pe.wait_ge(q_b_ready, 2 * pairs + 2)
                            pe.wait_ge(work_free, work.upto(1 if more else 0))
                        scores(pairs, par, i, next_row)
                        if p and i < NH:
                            sums(pairs - 1, i)
                        if i == 0:
                            next_qk(1)
                        if i == 1:
                            next_qk(2)
                        if i:
                            weigh(b, p, i - 1, next_row)
                        if i == 1:
                            next_qk(3)
                        next_row(6)
                    if more:
                        max_turn(pairs + 1)
                    weigh(b, p, NT - 1, lambda slot: None)
                for i in range(NT):
                    if not last:
                        v_tile(i)
                    if i in (2, 4):
                        sums(b * PAIRS + PAIRS - 1, i // 2 - 1)
                pe.wait_ge(hid_lo_done, ONE + (b + 1) * PAIRS * NH)
                for t in range(CT * NH):
                    o, cols = t // NH, slice(t % NH * HALF, (t % NH + 1) * HALF)
                    slot, piece = o // 2, o % 2
                    if t % (2 * NH) == 0:
                        n_load = (loads + 3 + slot) - (1 if last and slot else 0)
                        pe.wait_ge(ws_loaded[slot], n_load * 16)
                    product(next_tile(), [(w_s[:, slot, piece, w, j], hid[:, m, j, cols])
                                          for j in range(CT) for w, m in THREE]).then_inc(work_full, 1)

            with pe.Fori(0, B - 1) as b:
                batch1(b, False)
            batch1(B - 1, True)



def kernel(**inputs):
    import numpy as _np
    import concourse.bacc as _bacc
    from concourse import mybir as _mybir
    from concourse.bass_utils import run_bass_kernel_spmd as _run

    a = {k: _np.asarray(v) for k, v in inputs.items()}
    qkv, proj = a["L1_conv_w_qkv"], a["L1_conv_w_proj"]
    order = [qkv[i * C + p * P:i * C + (p + 1) * P] for p in range(CT) for i in range(2)]
    order += [proj[p * P:(p + 1) * P] for p in range(CT)]
    order += [qkv[2 * C + p * P:2 * C + (p + 1) * P] for p in range(CT)]
    w1 = _np.stack([w.T.reshape(CT, P, P).transpose(1, 0, 2) for w in order])
    host = {
        "x": a["x"].reshape(B, C, N),
        "wq_t": a["L0_conv_Wq"].T, "wv_t": a["L0_conv_Wv"].T, "wk": a["L0_conv_Wk"], "wo_t": a["L0_conv_Wo"].T,
        "bq0": a["L0_conv_bq"], "bv0": a["L0_conv_bv"], "bk0": a["L0_conv_bk"], "bo0": a["L0_conv_bo"],
        "gamma0": a["L0_conv_gamma"], "beta0": a["L0_conv_beta"],
        "gamma1": a["L1_conv_gamma"], "beta1": a["L1_conv_beta"],
        "w1": w1, "bqkv1": a["L1_conv_b_qkv"], "bproj1": a["L1_conv_b_proj"],
    }
    nc = _bacc.Bacc("TRN2", target_bir_lowering=False, num_devices=1)
    arrays, args = {}, []
    for name, v in host.items():
        v = _np.ascontiguousarray(v)
        arrays[name] = v
        args.append(nc.dram_tensor(name, v.shape, _mybir.dt.from_np(v.dtype), kind="ExternalInput").ap())
    args.append(nc.dram_tensor("out", (B, C, N), F32, kind="ExternalOutput").ap())
    build(nc, *args)
    r = _run(nc, [arrays], core_ids=[0])
    return r.results[0]["out"].reshape(B, C, 32, 32)
```

```python
from contextlib import ExitStack

import numpy as np

import concourse.bass as bass
from concourse import mybir

F32 = mybir.dt.float32
F32R = mybir.dt.float32r
BF16 = mybir.dt.bfloat16
ALU = mybir.AluOpType
ACT = mybir.ActivationFunctionType
AX_X = mybir.AxisListType.X

B, C, N = 8, 512, 1024
P = 128
HEADS = 8
D = C // HEADS
CT = C // P
NT = N // P
HALF = 512
NH = N // HALF
GROUPS = 32
GC = C // GROUPS
EPS = 1e-5
XT_SLOTS = 4
GRAN = 16
HI, LO = 0, 1
THREE = ((HI, HI), (HI, LO), (LO, HI))


class Arena:

    def __init__(self, tensor, size):
        self.tensor, self.size, self.at = tensor, size, 0

    def take(self, *shape):
        n = int(np.prod(shape))
        assert self.at + n <= self.size, (self.at, n, self.size)
        view = self.tensor[:, self.at:self.at + n]
        self.at += n
        if len(shape) > 1:
            names = "abcdef"[:len(shape)]
            view = view.rearrange(f"p ({' '.join(names)}) -> p {' '.join(names)}",
                                  **dict(zip(names[1:], shape[1:])))
        return view


def f(ap):
    return ap.bitcast(F32)


def build(nc, x, wq_t, wv_t, wk, wo_t, bq0, bv0, bk0, bo0, gamma0, beta0, gamma1, beta1, w1, bqkv1, bproj1, out):
    y_dram = nc.dram_tensor("y_dram", [B, C, N], F32).ap()
    w1_dram = nc.dram_tensor("w1_dram", [GRAN, P, 2, CT, P], F32R).ap()

    x_v = x.rearrange("b (j p) n -> b p j n", p=P)
    y_v = y_dram.rearrange("b (j p) n -> b p j n", p=P)
    out_v = out.rearrange("b (j p) n -> b p j n", p=P)

    def rows(w):
        return w.rearrange("(j p) m -> p j m", p=P)

    def column(v):
        return v.rearrange("(j p) -> p j", p=P)

    with ExitStack() as ctx:
        def sb(name, shape, dt):
            return ctx.enter_context(nc.sbuf_tensor(name, shape, dt))

        def sem(name):
            return ctx.enter_context(nc.semaphore(name))

        R_SIZE, A_SIZE = 152 * 256, 50 * 256
        r_all = sb("r_all", [P, R_SIZE], F32R)
        a_all = sb("a_all", [P, A_SIZE], F32)

        r0, a0 = Arena(r_all, R_SIZE), Arena(a_all, A_SIZE)
        w_q, w_v, w_k, w_o = (r0.take(2, CT, C) for _ in range(4))
        xs = r0.take(2, CT, N)
        xt = r0.take(XT_SLOTS, 2, C)
        gs = us = r0.take(2, CT, C)
        ts = a_s = r0.take(2, CT, C)
        ms = r0.take(2, CT, P)
        gran_s = r0.take(2, CT, P)
        x32 = a0.take(CT, N)
        y32 = a0.take(2, CT, HALF)
        stage32 = a0.take(2, C)
        two_rows = a0.take(C)
        bias_rows = a0.take(2, C)
        eye_wide = a0.take(C + C - P)
        gran32 = a0.take(CT, P)
        stats = a0.take(CT, B * NH, 6)
        group_avg = a0.take(P)
        w32 = y32.rearrange("p a j n -> p a (j n)").rearrange("p a (j m) -> p a j m", j=CT)

        r1, a1 = Arena(r_all, R_SIZE), Arena(a_all, A_SIZE)
        w_v1 = r1.take(CT, 2, CT, P)
        w_s = r1.take(2, 2, 2, CT, P)
        xn = r1.take(2, CT, N)
        q_a = r1.take(2, 2, N)
        k_a = r1.take(2, 2, N)
        k_b = r1.take(2, 2, N)
        q_b = r1.take(2, N)
        hid = r1.take(2, CT, N)
        v_t = a1.take(NT, C)
        probs = a1.take(2, 2, N)
        res32 = probs.rearrange("p a h n -> p (a h) n")
        y_half = a1.take(2, HALF)
        y_first = v_t.rearrange("p (j h) n -> p j (h n)", j=CT)
        p_sum = a1.take(2, N)
        o32 = a1.take(N)
        recip = a1.take(HALF)

        SMALL = 732
        small = sb("small", [P, SMALL], F32)
        s = Arena(small, SMALL)
        eye = s.take(P)
        ones64 = s.take(D)
        max2 = s.take(2, NT, NH)
        max_cols = s.take(4, 32)
        mean_var = s.take(CT, B, 2)
        bn_mv = s.take(CT, 2)
        bn_var = s.take(CT)
        root_tmp = s.take(CT * B)
        gn_in = s.take(CT, B)
        gn_mean = s.take(CT, B)
        x1_mean = s.take(CT, B)
        gn_tmp = s.take(CT, B)
        xn_scale, xn_bias = s.take(CT, B), s.take(CT, B)
        next_norm = s.take(2, CT)
        bn_scale, bn_bias, res_bias = s.take(CT), s.take(CT), s.take(CT)
        c_sum, c_vec, s_col = s.take(CT), s.take(CT), s.take(CT)
        bo_c, bk_c, g0_c, b0_c, g1_c, b1_c, bp_c = (s.take(CT) for _ in range(7))
        bqkv_c = s.take(3 * CT)
        bk_s = sb("bk_s", [P, CT, 2], F32R)
        s_s = sb("s_s", [P, CT, 2], F32R)
        mask = sb("mask", [64, NT, P], BF16)

        psum = [ctx.enter_context(nc.psum_tensor(f"psum{i}", [P, 2, HALF], F32)) for i in range(4)]

        def bank(i):
            return psum[i // 2][:, i % 2, :]

        w_loaded = [sem("w_loaded0"), sem("w_loaded1")]
        consts_loaded = sem("consts_loaded")
        x_loaded = [sem(f"x_loaded{h}") for h in range(NH)]
        y_stored = [sem(f"y_stored{h}") for h in range(NH)]
        w_hi_done = sem("w_hi_done")
        w_lo_done = sem("w_lo_done")
        consts_ready = sem("consts_ready")
        dve_step = sem("dve_step")
        pool_step = sem("pool_step")
        x_hi_done = sem("x_hi_done")
        x_lo_done = sem("x_lo_done")
        ring_full = sem("ring_full")
        ring_free = sem("ring_free")
        hi_done = sem("hi_done")
        lo_done = sem("lo_done")
        xt_used = sem("xt_used")
        x_summed = sem("x_summed")
        g_full = sem("g_full")
        mirror_full = sem("mirror_full")
        mirror_hi_done, mirror_lo_done = sem("mirror_hi_done"), sem("mirror_lo_done")
        row_full = sem("row_full")
        row_ready = sem("row_ready")
        m_full = sem("m_full")
        m_split = sem("m_split")
        c_full = sem("c_full")
        c_ready = sem("c_ready")
        y_full = sem("y_full")
        y_ready = sem("y_ready")
        y_counted = sem("y_counted")
        stats_ready = sem("stats_ready")
        gran_loaded = sem("gran_loaded")
        gran_split = sem("gran_split")
        gran_stored = sem("gran_stored")
        pads_ready = sem("pads_ready")
        gn_moved = sem("gn_moved")
        gn_averaged = sem("gn_averaged")
        norm_ready = sem("norm_ready")
        var_ready = sem("var_ready")
        root_ready = sem("root_ready")
        wv1_loaded = sem("wv1_loaded")
        ws_loaded = [sem("ws_loaded0"), sem("ws_loaded1")]
        y_first_loaded = sem("y_first_loaded")
        y_half_loaded = [sem("y_half_loaded0"), sem("y_half_loaded1")]
        v_first_full, v_first_done = sem("v_first_full"), sem("v_first_done")
        end_sums_full, end_sums_read = sem("end_sums_full"), sem("end_sums_read")
        next_norm_ready = sem("next_norm_ready")
        xn_made = sem("xn_made")
        xn_hi_done = sem("xn_hi_done")
        xn_lo_done = sem("xn_lo_done")
        work_full = sem("work_full")
        work_free = sem("work_free")
        qk_hi_done = sem("qk_hi_done")
        k_twice = sem("k_twice")
        max_ready = sem("max_ready")
        q_b_ready = sem("q_b_ready")
        scores_full = sem("scores_full")
        probs_ready = sem("probs_ready")
        pv_done = sem("pv_done")
        sum_step = sem("sum_step")
        last_sums = sem("last_sums")
        o_ready = sem("o_ready")
        o_normed = sem("o_normed")
        hid_hi_done = sem("hid_hi_done")
        hid_lo_done = sem("hid_lo_done")
        res_loaded = sem("res_loaded")
        res_scaled = sem("res_scaled")
        out_stored = [sem("out_stored0"), sem("out_stored1")]

        block = ctx.enter_context(nc.Block())

        T0, U0, A0, RING0 = NT, NT + CT, NT + 2 * CT, NT + 3 * CT
        G_S, T_S, U_S, A_S, SPLITS = NT, NT + CT, NT + 2 * CT, NT + 3 * CT, NT + 4 * CT
        G_FROM = [min(g, CT - 2) * P for g in range(CT)]
        AHEAD = 3

        def ring_bank(t):
            return bank(4 + t % 4)

        PAIRS = CT
        QK, SMAX, SUMS = 2 * NH, 2 * NT * NH, NH
        WORK0 = QK + SMAX + 1
        WORK = PAIRS * (QK + SMAX + 1) + (PAIRS - 1) * SUMS + NT + CT * NH
        assert WORK % 2 == 0
        NEXT = QK + SMAX + 1

        def qk_used(b, p):
            return b * WORK + (WORK0 + p * (NEXT + SUMS) + QK)

        def sums_used(b, p, last):
            if p == 0:
                return b * WORK + (WORK0 - CT * NH - (NT - 6))
            return b * WORK + (WORK0 + p * (NEXT + SUMS) + (0 if last and p == PAIRS - 1 else QK // 2))

        def proj_used(b, t, last):
            return b * WORK + (WORK0 + WORK - CT * NH - (NEXT + NT if last else 0) + t)

        ROW_PLACES = ((), (), (8, 9, 9)) + 4 * ((2, 4, 7, 8, 8, 9),) + ((2, 4, 7, 8, 8),)
        ROWS = [len(places) for places in ROW_PLACES]
        assert len(ROWS) == NT and sum(ROWS) == SMAX
        NORM_STEP = (1, 2, 3, 3, 4, 5, 5, 6)
        LO_ROW = (3, 6, 9, 12, 16, 20, 24, 27)
        HID_ROW = 5

        def proj_tiles(last):
            if last:
                return [(o, half) for half in range(NH) for o in range(CT)]
            return [(o, half) for o in range(CT) for half in range(NH)]

        SCALE = 1.0 / float(np.sqrt(D))

        ONE = 1

        LAST_SUMS = ONE + (B * PAIRS - 1) * 2 * (NT - 1)

        class Tally:

            def __init__(self):
                self.base, self.n, self.started = 0, 0, False

            def start(self, b):
                self.base, self.n, self.started = b * WORK, WORK0, True

            def next(self):
                self.n += 1
                return self.base + self.n, bank(6 + self.n % 2)

            def upto(self, n=0):
                return self.base + self.n - n

        def mirror(part, i):
            n = CT - 1 - i
            of = bank(part)[:, 0:n * P].rearrange("p (g c) -> p g c", c=P)
            return gs[:, part, i + 1:CT, i * P:(i + 1) * P], of

        @block.sync
        def _(sp):
            for h in range(NH):
                sp.dma_start(x32[:, :, h * HALF:(h + 1) * HALF], x_v[0, :, :, h * HALF:(h + 1) * HALF]).then_inc(x_loaded[h], 16)
            weights = (wv_t, wq_t, wo_t, wk)
            for w in range(2):
                sp.dma_start(w32[:, w], rows(weights[w])).then_inc(w_loaded[w], 16)
            for i, (to, of) in enumerate((
                    (bias_rows[:, 0], bq0.rearrange("(a n) -> a n", a=1).to_broadcast([P, C])),
                    (bias_rows[:, 1], bv0.rearrange("(a n) -> a n", a=1).to_broadcast([P, C])))):
                sp.dma_start(to, of).then_inc(consts_loaded, 16)
            for to, of in ((bo_c, bo0), (bk_c, bk0), (g0_c, gamma0), (b0_c, beta0), (g1_c, gamma1), (b1_c, beta1),
                           (bp_c, bproj1), (bqkv_c, bqkv1)):
                with nc.allow_non_contiguous_dma(reason="a bias column, 2 KB in all"):
                    sp.dma_start(to, column(of)).then_inc(consts_loaded, 16)
            for w in range(2, 4):
                sp.wait_ge(w_lo_done, w - 1)
                sp.dma_start(w32[:, w % 2], rows(weights[w])).then_inc(w_loaded[w % 2], 16)
            def store_y(b):
                for h in range(NH):
                    sp.wait_ge(y_ready, b * NH * CT + (h + 1) * CT)
                    sp.dma_start(y_v[b, :, :, h * HALF:(h + 1) * HALF], y32[:, h]).then_inc(y_stored[h], 16)

            def x_free(b):
                sp.wait_ge(x_lo_done, (b + 1) * CT)
                sp.wait_ge(ring_full, b * RING0 + NT)

            with sp.Fori(0, B - 1) as b:
                x_free(b)
                for h in range(NH):
                    cols = slice(h * HALF, (h + 1) * HALF)
                    sp.dma_start(x32[:, :, cols], x_v[b + 1, :, :, cols]).then_inc(x_loaded[h], 16)
                store_y(b)

            x_free(B - 1)
            for h in range(NH):
                sp.wait_ge(y_stored[h], 16 * (B - 1))
            sp.dma_start(y_first, y_v[0]).then_inc(y_first_loaded, 16)
            sp.wait_ge(m_full, B * CT)
            sp.wait_ge(gran_stored, GRAN * 16)

            def pieces(first, n):
                return f(w1_dram[first:first + n].rearrange("g p a j m -> p g (a j m)"))

            def load_stream(slot, first):
                sp.dma_start(f(w_s[:, slot].rearrange("p g a j m -> p g (a j m)")), pieces(first, 2)).then_inc(ws_loaded[slot], 16)

            def load_y(b, us_):
                for u in us_:
                    if u >= 2:
                        sp.wait_ge(xn_lo_done, b * NH * CT + u - 1)
                    src = y_v[b, :, u // NH, u % NH * HALF:(u % NH + 1) * HALF]
                    sp.dma_start(y_half[:, u % 2], src).then_inc(y_half_loaded[u % 2], 16)

            load_stream(1, 0)
            sp.dma_start(f(w_v1.rearrange("p g a j m -> p g (a j m)")), pieces(3 * CT, CT)).then_inc(wv1_loaded, 16)
            load_stream(0, 2)
            store_y(B - 1)
            for h in range(NH):
                sp.wait_ge(y_stored[h], 16 * B)

            for half in out_stored:
                sp.sem_inc(half, ONE)
            sp.wait_ge(work_full, QK)
            load_stream(1, 4)

            def batch1(b, last):
                sp.wait_ge(work_full, qk_used(b, 0))
                load_stream(0, 6)
                sp.wait_ge(work_full, qk_used(b, 1))
                load_stream(1, 10 if last else 0)
                if not last:
                    load_y(b + 1, range(2))
                if not last:
                    load_y(b + 1, range(2, NH * CT))
                sp.wait_ge(work_full, qk_used(b, 2))
                load_stream(0, 8)
                if not last:
                    sp.wait_ge(work_full, qk_used(b, 3))
                    load_stream(1, 10)
                sp.wait_ge(pv_done, ONE + (b + 1) * PAIRS * NT)
                if last:
                    sp.wait_ge(sum_step, LAST_SUMS + NT - 1)
                    sp.wait_ge(last_sums, NT - 1)
                else:
                    sp.wait_ge(sum_step, ONE + (b + 1) * PAIRS * 2 * (NT - 1))
                sp.dma_start(res32, y_v[b]).then_inc(res_loaded, 16)
                for o in range(CT):
                    sp.wait_ge(work_free, proj_used(b, proj_tiles(last).index((o, NH - 1)) + 1, last))
                    sp.dma_start(out_v[b, :, o], res32[:, o]).then_inc(out_stored[o // 2], 16)
                    if not last and o % 2:
                        load_stream(o // 2, 2 + o // 2 * 2)

            with sp.Fori(0, B - 1) as b:
                batch1(b, False)
            batch1(B - 1, True)
            for half in out_stored:
                sp.wait_ge(half, ONE + B * CT // 2 * 16)

        @block.gpsimd
        def _(pool):
            pool.memset(eye_wide, 0.0).then_inc(pool_step, 1)
            pool.memset(eye, 0.0).then_inc(pool_step, 1)
            pool.memset(mask[:, :, :], 0.0).then_inc(pool_step, 1)
            pool.memset(group_avg, 1.0 / GC).then_inc(pool_step, 1)
            pool.memset(ones64, 1.0).then_inc(pool_step, 1)
            pool.memset(f(ms), 0.0).then_inc(pool_step, 1)
            pool.wait_ge(pool_step, 6)
            mid = eye_wide[:, C - P:C]
            pool.affine_select(out=mid, in_=mid, compare_op=ALU.not_equal, fill=1.0, base=0,
                               pattern=[[-1, P]], channel_multiplier=1).then_inc(pool_step, 1)
            pool.wait_ge(pool_step, 7)
            pool.affine_select(out=eye, in_=eye, compare_op=ALU.not_equal, fill=1.0, base=0,
                               pattern=[[-1, P]], channel_multiplier=1).then_inc(pool_step, 1)
            for h in range(2):
                pool.wait_ge(pool_step, 8 + h)
                pool.affine_select(out=mask[32 * h:32 * h + 32, :, :], in_=mask[32 * h:32 * h + 32, :, :],
                                   compare_op=ALU.not_equal, fill=-1.0, base=0,
                                   pattern=[[-1, NT], [0, P]], channel_multiplier=1).then_inc(pool_step, 1)
            blocks = group_avg.rearrange("p (g c) -> p g c", c=GC)
            pool.wait_ge(pool_step, 10)
            pool.affine_select(out=blocks, in_=blocks, compare_op=ALU.is_ge, fill=0.0, base=0,
                               pattern=[[-GC, P // GC], [0, GC]], channel_multiplier=1).then_inc(pool_step, 1)
            pool.wait_ge(pool_step, 11)
            pool.affine_select(out=blocks, in_=blocks, compare_op=ALU.is_ge, fill=0.0, base=GC - 1,
                               pattern=[[GC, P // GC], [0, GC]], channel_multiplier=-1).then_inc(pool_step, 1)
            pool.wait_ge(pool_step, 12)
            pool.sem_inc(consts_ready, 1)
            with pool.Fori(0, GRAN) as g:
                pool.dma_start(gran32, w1[g]).then_inc(gran_loaded, 16)
                pool.wait_ge(gran_loaded, g * 16 + 16)
                pool.tensor_tensor(gran_s[:, HI], gran32, ones64[:, 0:1].unsqueeze(1).to_broadcast([P, CT, P]), ALU.mult).then_inc(gran_split, 1)
                pool.wait_ge(gran_split, g * 2 + 1)
                pool.tensor_tensor(gran_s[:, LO], gran32, f(gran_s[:, HI]), ALU.subtract).then_inc(gran_split, 1)
                pool.wait_ge(gran_split, g * 2 + 2)
                pool.dma_start(w1_dram[g], gran_s).then_inc(gran_stored, 16)
                pool.wait_ge(gran_stored, g * 16 + 16)

            pool.sem_inc(sum_step, ONE)
            pool.wait_ge(y_full, B * NH * CT)
            n = 0
            for h in range(2):
                pad = slice(D - h * D, 2 * D - h * D)
                pick = slice(D - h * D, D - h * D + NT)
                for to, value in ((q_b[pad, h], 0.0), (k_b[pad, 0, h], 0.0), (k_b[pad, 1, h], 0.0),
                                  (k_b[pick, 0, h], 1.0), (k_b[pick, 1, h], 1.0)):
                    if n:
                        pool.wait_ge(pads_ready, n)
                    pool.memset(f(to), value).then_inc(pads_ready, 1)
                    n += 1

            def batch1(b, last):
                for p in range(PAIRS):
                    last_pair = last and p == PAIRS - 1
                    for i in range(1, NT):
                        for h in range(1 if last_pair else 2):
                            if i == 1 and h == 0:
                                pool.wait_ge(work_full, sums_used(b, p, last))
                            pool.wait_ge(probs_ready, ONE + b * PAIRS * 2 * NT + p * 2 * NT + 2 * i + h + 1)
                            pool.wait_ge(sum_step, ONE + b * PAIRS * 2 * (NT - 1) + p * 2 * (NT - 1) +
                                         (i - 1 if last_pair else 2 * (i - 1) + h))
                            pool.tensor_tensor(p_sum[:, h], probs[:, 0, h] if i == 1 else p_sum[:, h],
                                               probs[:, i % 2, h], ALU.add).then_inc(sum_step, 1)

            with pool.Fori(0, B - 1) as b:
                batch1(b, False)
            batch1(B - 1, True)

        @block.scalar
        def _(act):
            def hi(to, of):
                act.activation(to, of, ACT.Copy).then_inc(hi_done, 1)

            def w_hi(w):
                act.wait_ge(w_loaded[w % 2], 16 * (w // 2 + 1))
                act.activation((w_v, w_q, w_o, w_k)[w][:, HI], w32[:, w % 2], ACT.Copy).then_inc(w_hi_done, 1)

            def xt_hi(b, n, first=False):
                act.wait_ge(ring_full, b * RING0 + n + 1)
                if not first or n >= XT_SLOTS:
                    act.wait_ge(xt_used, b * NT + n - XT_SLOTS + 1)
                hi(xt[:, n % XT_SLOTS, HI], ring_bank(n))

            def batch(b, first, last):
                for n in range(0 if first else AHEAD, NT):
                    xt_hi(b, n, first)
                    if 3 <= n < 3 + CT:
                        if n == 3:
                            for h in range(NH):
                                act.wait_ge(x_loaded[h], b * 16 + 16)
                            if not first:
                                act.wait_ge(y_full, b * NH * CT)
                        act.activation(xs[:, HI, n - 3], x32[:, n - 3], ACT.Copy).then_inc(x_hi_done, 1)
                    if first and n in (3, 5):
                        w_hi(n // 2 - 1)
                for g in range(CT):
                    act.wait_ge(g_full, b * CT + g + 1)
                    hi(gs[:, HI, g, G_FROM[g]:], bank(g)[:, G_FROM[g]:])
                for i in range(2):
                    act.wait_ge(mirror_full, b * 4 + 2 * i + 1)
                    act.activation(*mirror(HI, i), ACT.Copy).then_inc(mirror_hi_done, 1)
                if first:
                    w_hi(2)
                for o in range(CT):
                    act.wait_ge(ring_free, b * 2 * CT + o + 1)
                    hi(ts[:, HI, o], stage32[:, o % 2])
                if first:
                    w_hi(3)
                for g in range(CT):
                    act.wait_ge(ring_full, b * RING0 + U0 + g + 1)
                    hi(us[:, HI, g], ring_bank(U0 + g))
                for g in range(CT):
                    act.wait_ge(ring_free, b * 2 * CT + CT + g + 1)
                    hi(a_s[:, HI, g], stage32[:, g % 2])
                act.wait_ge(c_ready, b + 1)
                for h in range(NH):
                    act.wait_ge(y_stored[h], b * 16)
                    act.wait_ge(y_counted, b * NH * CT)
                    for o in range(CT):
                        act.wait_ge(y_full, b * NH * CT + h * CT + o + 1)
                        act.activation(y32[:, h, o], bank(o), ACT.Identity, bias=c_vec[:, o:o + 1]).then_inc(y_ready, 1)
                    if h == 0 and not last:
                        for n in range(AHEAD):
                            xt_hi(b + 1, n)

            batch(0, True, False)
            with act.Fori(1, B - 1) as b:
                batch(b, False, False)
            batch(B - 1, False, True)

            work = Tally()

            def norm_half(b, u, first=False):
                j, half = (u % CT, u // CT) if first else (u // NH, u % NH)
                cols = slice(half * HALF, (half + 1) * HALF)
                if not first:
                    act.wait_ge(y_half_loaded[u % 2], (b - 1) * (NH * CT // 2 * 16) + (u // 2 + 1) * 16)
                    act.activation(y_half[:, u % 2], y_half[:, u % 2], ACT.Identity, scale=next_norm[:, 0, j:j + 1],
                                   bias=next_norm[:, 1, j:j + 1]).then_inc(xn_made, 1)
                act.wait_ge(xn_made, b * NH * CT + u + 1)
                of = y_first[:, j, cols] if first else y_half[:, u % 2]
                act.activation(xn[:, HI, j, cols], of, ACT.Copy).then_inc(xn_hi_done, 1)

            def qk_hi(b, pair, par, i, count):
                n, ps = work.next()
                act.wait_ge(work_full, n)
                of_k, cols = i // 2, slice(i % 2 * HALF, (i % 2 + 1) * HALF)
                bias = bqkv_c[:, of_k * CT + pair:of_k * CT + pair + 1]
                to = (q_a, k_a)[of_k]
                for h in range(2):
                    rows_ = slice(h * D, h * D + D)
                    act.activation(to[rows_, par, h, cols], ps[rows_, :], ACT.Identity, bias=bias[rows_]).then_inc(qk_hi_done, 1)
                if of_k:
                    for h in range(2):
                        act.wait_ge(qk_hi_done, 2 * (count + i) + h + 1)
                        rows_, others = slice(h * D, h * D + D), slice(D - h * D, 2 * D - h * D)
                        act.activation(k_a[others, par, h, cols], f(k_a[rows_, par, h, cols]), ACT.Copy).then_inc(k_twice, 1)

            def q_b_hi(par):
                for h in range(2):
                    rows_ = slice(h * D, h * D + D)
                    act.activation(q_b[rows_, h], f(q_a[rows_, par, h]), ACT.Copy).then_inc(q_b_ready, 1)

            def hid_hi(b, pair, h):
                cols = slice(h * HALF, (h + 1) * HALF)
                act.wait_ge(o_normed, ONE + b * PAIRS * NH + pair * NH + h + 1)
                act.activation(hid[:, HI, pair, cols], o32[:, cols], ACT.Identity,
                               bias=bqkv_c[:, 2 * CT + pair:2 * CT + pair + 1]).then_inc(hid_hi_done, 1)

            for i, (v, root) in enumerate(((bn_var, bn_scale), (gn_in, gn_tmp))):
                act.wait_ge(var_ready, i + 1)
                act.activation(root, v, ACT.Sqrt).then_inc(root_ready, 1)
            act.sem_inc(probs_ready, ONE)
            act.sem_inc(o_ready, ONE)
            act.wait_ge(norm_ready, 1)
            for u in range(NH * CT):
                norm_half(0, u, True)
            for i in range(QK):
                qk_hi(0, 0, 0, i, 0)
            q_b_hi(0)
            for i in range(NT):
                act.wait_ge(v_first_full, i + 1)
                act.activation(v_t[:, i], bank(i % CT), ACT.Copy).then_inc(v_first_done, 1)

            def batch1(b, last):
                work.start(b)
                for p in range(PAIRS):
                    more = p < PAIRS - 1 or not last
                    par, pairs = (p + 1) % 2, b * PAIRS + p

                    def next_qk(i):
                        if more:
                            qk_hi(b, (p + 1) % PAIRS, par, i, (pairs + 1) * QK)

                    next_qk(0)
                    for i in range(NT):
                        for h in range(2):
                            act.wait_ge(scores_full, pairs * 2 * NT + 2 * i + h + 1)
                            if h == 0 and i >= 2:
                                act.wait_ge(pv_done, ONE + pairs * NT + i - 1)
                            if i >= 2 and not more:
                                act.wait_ge((sum_step, last_sums)[h], (LAST_SUMS, 0)[h] + max(i - 2, 1))
                            elif i >= 2:
                                act.wait_ge(sum_step, ONE + pairs * 2 * (NT - 1) + 2 * (max(i - 2, 1) - 1) + h + 1)
                            elif p == 0 and h == 0:
                                if i == 0:
                                    act.wait_ge(sum_step, ONE + pairs * 2 * (NT - 1))
                                    act.wait_ge(pv_done, ONE + pairs * NT)
                                act.wait_ge(out_stored[i], ONE + b * CT // 2 * 16)
                            elif p:
                                act.wait_ge(sum_step, ONE + pairs * 2 * (NT - 1) - 2 * (1 - i) - 1 + h)
                            act.activation(probs[:, i % 2, h], psum[h][:, :, :].rearrange("p a n -> p (a n)"), ACT.Exp,
                                           scale=SCALE).then_inc(probs_ready, 1)
                        if p and i < NH:
                            work.next()
                        if i == 0:
                            next_qk(1)
                        if i == 1:
                            next_qk(2)
                            if p:
                                hid_hi(b, p - 1, 0)
                            next_qk(3)
                            if p:
                                hid_hi(b, p - 1, 1)
                        if more:
                            for _ in range(ROWS[i]):
                                work.next()
                        if p == 2 and not last:
                            if i == 1:
                                act.wait_ge(work_full, qk_used(b, 2))
                                act.wait_ge(next_norm_ready, 2 * b + 2)
                            for u in range(NH * CT):
                                if NORM_STEP[u] == i:
                                    norm_half(b + 1, u)
                    if more:
                        work.next()
                        q_b_hi(par)
                    act.wait_ge(hid_lo_done, ONE + pairs * NH)
                    act.wait_ge(pv_done, ONE + (pairs + 1) * NT)
                    act.activation(o32, psum[2][:, :, :].rearrange("p a n -> p (a n)"), ACT.Copy).then_inc(o_ready, 1)
                for h in range(NH):
                    hid_hi(b, PAIRS - 1, h)
                act.wait_ge(res_loaded, (b + 1) * 16)
                for o in range(CT):
                    act.activation(res32[:, o], res32[:, o], ACT.Identity, scale=bn_scale[:, o:o + 1],
                                   bias=res_bias[:, o:o + 1]).then_inc(res_scaled, 1)

            with act.Fori(0, B - 1) as b:
                batch1(b, False)
            batch1(B - 1, True)

        @block.vector
        def _(dve):
            def split_w(w):
                to = (w_v, w_q, w_o, w_k)[w]
                dve.wait_ge(w_hi_done, w + 1)
                dve.tensor_tensor(to[:, LO], w32[:, w % 2], f(to[:, HI]), ALU.subtract).then_inc(w_lo_done, 1)

            dve.wait_ge(consts_ready, 1)
            FIRST, STEPS = 2, 2 * CT + 1

            def lo(to, of, hi_part):
                dve.tensor_tensor(to, of, f(hi_part), ALU.subtract).then_inc(lo_done, 1)

            def xt_lo(b, n):
                dve.wait_ge(hi_done, b * SPLITS + n + 1)
                to = xt[:, n % XT_SLOTS]
                lo(to[:, LO], ring_bank(n), to[:, HI])

            def batch_stats(b):
                for j in range(CT):
                    dve.bn_aggr(mean_var[:, j, b], stats[:, j, b * NH:(b + 1) * NH].rearrange("p a k -> p (a k)")).then_inc(stats_ready, 1)

            def batch(b, first, last):
                for n in range(0 if first else AHEAD, NT):
                    xt_lo(b, n)
                    j = n - 3
                    if 0 <= j < CT:
                        if j == 0:
                            dve.wait_ge(x_summed, b * (CT + 2))
                            for h in range(NH):
                                dve.wait_ge(x_loaded[h], b * 16 + 16)
                        dve.reduce_sum(s_col[:, j:j + 1], x32[:, j], AX_X).then_inc(x_summed, 1)
                        dve.wait_ge(x_hi_done, b * CT + j + 1)
                        dve.tensor_tensor(xs[:, LO, j], x32[:, j], f(xs[:, HI, j]), ALU.subtract).then_inc(x_lo_done, 1)
                    if first and n in (3, 5):
                        split_w(n // 2 - 1)
                dve.wait_ge(x_summed, b * (CT + 2) + CT)
                dve.tensor_copy(s_s[:, :, HI], s_col).then_inc(x_summed, 1)
                dve.wait_ge(x_summed, b * (CT + 2) + CT + 1)
                dve.tensor_tensor(s_s[:, :, LO], s_col, f(s_s[:, :, HI]), ALU.subtract).then_inc(x_summed, 1)
                for g in range(CT):
                    dve.wait_ge(hi_done, b * SPLITS + G_S + g + 1)
                    lo(gs[:, LO, g, G_FROM[g]:], bank(g)[:, G_FROM[g]:], gs[:, HI, g, G_FROM[g]:])
                for i in range(2):
                    dve.wait_ge(mirror_full, b * 4 + 2 * i + 2)
                    dve.tensor_copy(*mirror(LO, i)).then_inc(mirror_lo_done, 1)
                if first:
                    split_w(2)
                    dve.wait_ge(consts_loaded, 10 * 16)
                    dve.tensor_copy(bk_s[:, :, HI], bk_c).then_inc(dve_step, 1)
                    dve.wait_ge(dve_step, 1)
                    dve.tensor_tensor(bk_s[:, :, LO], bk_c, f(bk_s[:, :, HI]), ALU.subtract).then_inc(dve_step, 1)

                def t_lo(o):
                    dve.wait_ge(hi_done, b * SPLITS + T_S + o + 1)
                    lo(ts[:, LO, o], stage32[:, o % 2], ts[:, HI, o])

                for o in range(CT):
                    dve.wait_ge(ring_full, b * RING0 + T0 + o + 1)
                    if not first or o >= 2:
                        dve.wait_ge(lo_done, b * SPLITS + (T_S + o - 1 if o >= 2 else 0))
                    dve.scalar_tensor_tensor(out=stage32[:, o % 2], in0=bias_rows[:, 1], scalar=s_col[:, o:o + 1],
                                             in1=ring_bank(T0 + o), op0=ALU.mult, op1=ALU.add).then_inc(ring_free, 1)
                    if o:
                        t_lo(o - 1)
                dve.wait_ge(row_full, 2 * b + 1)
                dve.scalar_tensor_tensor(out=two_rows[0:2], in0=bias_rows[0:2, 1], scalar=N / 2, in1=bank(3)[0:2, :],
                                         op0=ALU.mult, op1=ALU.add).then_inc(row_ready, 1)
                t_lo(CT - 1)
                if first:
                    split_w(3)
                for g in range(CT):
                    dve.wait_ge(m_full, b * CT + g + 1)
                    if g == 0:
                        dve.wait_ge(m_split, b * 2 * CT)
                    for e in range(2):
                        part = slice(e * D, e * D + D)
                        of = bank(g)[part, g % 2 * P + e * D:g % 2 * P + e * D + D]
                        dve.tensor_copy(ms[part, HI, g, part], of).then_inc(dve_step, 1)
                    dve.wait_ge(dve_step, b * STEPS + FIRST + 2 * g + 2)
                    for e in range(2):
                        part = slice(e * D, e * D + D)
                        of = bank(g)[part, g % 2 * P + e * D:g % 2 * P + e * D + D]
                        dve.tensor_tensor(ms[part, LO, g, part], of, f(ms[part, HI, g, part]),
                                          ALU.subtract).then_inc(m_split, 1)
                for g in range(CT):
                    dve.wait_ge(hi_done, b * SPLITS + U_S + g + 1)
                    lo(us[:, LO, g], ring_bank(U0 + g), us[:, HI, g])
                dve.wait_ge(row_full, 2 * b + 2)
                dve.wait_ge(row_ready, 2 * b + 1)
                dve.tensor_copy(two_rows[0:2], bank(3)[0:2, :]).then_inc(row_ready, 1)

                def a_lo(g):
                    dve.wait_ge(hi_done, b * SPLITS + A_S + g + 1)
                    lo(a_s[:, LO, g], stage32[:, g % 2], a_s[:, HI, g])

                for g in range(CT):
                    dve.wait_ge(ring_full, b * RING0 + A0 + g + 1)
                    dve.wait_ge(lo_done, b * SPLITS + A_S + max(0, g - 1))
                    dve.tensor_tensor(stage32[:, g % 2], ring_bank(A0 + g), eye_wide[:, C - P - g * P:2 * C - P - g * P],
                                      ALU.add).then_inc(ring_free, 1)
                    if g:
                        a_lo(g - 1)
                a_lo(CT - 1)
                dve.wait_ge(c_full, b + 1)
                dve.wait_ge(c_ready, b)
                dve.tensor_copy(c_sum, bank(3)[:, 0:2 * CT].rearrange("p (o t) -> p o t", t=2)[:, :, 0]).then_inc(dve_step, 1)
                dve.wait_ge(dve_step, b * STEPS + FIRST + STEPS)
                dve.wait_ge(y_ready, b * NH * CT)
                dve.tensor_tensor(c_vec, c_sum, bo_c, ALU.add).then_inc(c_ready, 1)
                if last:
                    dve.wait_ge(y_counted, b * NH * CT)
                    for before in range(B - 1):
                        batch_stats(before)
                for h in range(NH):
                    for o in range(CT):
                        dve.wait_ge(y_ready, b * NH * CT + h * CT + o + 1)
                        if first or last:
                            to = stats[:, o, b * NH + h, :]
                        else:
                            to = stats[:, o, bass.ds(b * NH + h, 1), :].rearrange("p a k -> p (a k)")
                        dve.bn_stats(to, y32[:, h, o]).then_inc(y_counted, 1)
                    if h == 0 and not last:
                        for n in range(AHEAD):
                            xt_lo(b + 1, n)

            batch(0, True, False)
            with dve.Fori(1, B - 1) as b:
                batch(b, False, False)
            batch(B - 1, False, True)

            steps = FIRST + B * STEPS

            def then(ins):
                nonlocal steps
                steps += 1
                ins.then_inc(dve_step, 1)
                dve.wait_ge(dve_step, steps)

            def invert(root, v, tmp):
                then(dve.reciprocal(root, root))
                then(dve.tensor_tensor(tmp, root, root, ALU.mult))
                then(dve.tensor_tensor(tmp, tmp, v, ALU.mult))
                then(dve.tensor_scalar(tmp, tmp, -0.5, 1.5, ALU.mult, ALU.add))
                then(dve.tensor_tensor(root, root, tmp, ALU.mult))

            def wide(v):
                return v.unsqueeze(2).to_broadcast([P, CT, B])

            dve.wait_ge(y_counted, B * NH * CT)
            for j in range(CT):
                dve.bn_aggr(bn_mv[:, j], stats[:, j].rearrange("p a k -> p (a k)")).then_inc(stats_ready, 1)
            batch_stats(B - 1)
            dve.wait_ge(stats_ready, CT * (B + 1))
            dve.tensor_scalar(bn_var, bn_mv[:, :, 1], EPS, None, ALU.add).then_inc(var_ready, 1)
            dve.wait_ge(root_ready, 1)
            invert(bn_scale, bn_var, root_tmp[:, 0:CT])
            then(dve.tensor_tensor(bn_scale, bn_scale, g0_c, ALU.mult))
            then(dve.tensor_tensor(bn_bias, bn_mv[:, :, 0], bn_scale, ALU.mult))
            then(dve.tensor_tensor(bn_bias, b0_c, bn_bias, ALU.subtract))
            then(dve.tensor_tensor(res_bias, bn_bias, bp_c, ALU.add))
            then(dve.tensor_tensor(x1_mean, mean_var[:, :, :, 0], wide(bn_scale), ALU.mult))
            dve.tensor_tensor(x1_mean, x1_mean, wide(bn_bias), ALU.add).then_inc(gn_moved, 1)
            dve.wait_ge(gn_moved, 1)
            dve.wait_ge(gn_averaged, 1)
            then(dve.tensor_copy(gn_mean, bank(6)[:, 0:CT * B].rearrange("p (j b) -> p j b", b=B)))
            then(dve.tensor_tensor(gn_tmp, x1_mean, gn_mean, ALU.subtract))
            then(dve.tensor_tensor(gn_tmp, gn_tmp, gn_tmp, ALU.mult))
            then(dve.tensor_tensor(gn_in, mean_var[:, :, :, 1], wide(bn_scale), ALU.mult))
            then(dve.tensor_tensor(gn_in, gn_in, wide(bn_scale), ALU.mult))
            dve.tensor_tensor(gn_in, gn_in, gn_tmp, ALU.add).then_inc(gn_moved, 1)
            dve.wait_ge(gn_averaged, 2)
            dve.tensor_scalar(gn_in, bank(7)[:, 0:CT * B].rearrange("p (j b) -> p j b", b=B), EPS, None, ALU.add).then_inc(var_ready, 1)
            dve.wait_ge(root_ready, 2)
            invert(gn_tmp, gn_in, root_tmp.rearrange("p (j b) -> p j b", b=B))
            then(dve.tensor_tensor(gn_tmp, gn_tmp, wide(g1_c), ALU.mult))
            then(dve.tensor_tensor(xn_scale, gn_tmp, wide(bn_scale), ALU.mult))
            then(dve.tensor_tensor(xn_bias, wide(bn_bias), gn_mean, ALU.subtract))
            then(dve.tensor_tensor(xn_bias, xn_bias, gn_tmp, ALU.mult))
            then(dve.memset(max_cols, 0.0))
            dve.tensor_tensor(xn_bias, xn_bias, wide(b1_c), ALU.add).then_inc(norm_ready, 1)

            work = Tally()

            def norm_lo(b, u):
                j, cols = u // NH, slice(u % NH * HALF, (u % NH + 1) * HALF)
                dve.wait_ge(xn_hi_done, b * NH * CT + u + 1)
                dve.tensor_tensor(xn[:, LO, j, cols], y_half[:, u % 2], f(xn[:, HI, j, cols]), ALU.subtract).then_inc(xn_lo_done, 1)

            def qk_lo(pair, par, i, count):
                n, ps = work.next()
                of_k, cols = i // 2, slice(i % 2 * HALF, (i % 2 + 1) * HALF)
                bias = bqkv_c[:, of_k * CT + pair:of_k * CT + pair + 1]
                for h in range(2):
                    rows_, others = slice(h * D, h * D + D), slice(D - h * D, 2 * D - h * D)
                    to = k_b[rows_, par, h, cols] if of_k else q_a[others, par, h, cols]
                    dve.wait_ge(qk_hi_done, 2 * (count + i) + h + 1)
                    ins = dve.scalar_tensor_tensor(out=to, in0=ps[rows_, :], scalar=bias[rows_],
                                                   in1=f((q_a, k_a)[of_k][rows_, par, h, cols]),
                                                   op0=ALU.add, op1=ALU.subtract)
                ins.then_inc(work_free, 1)

            def max_tile(t):
                n, ps = work.next()
                h, tile, half = t // (NT * NH), t // NH % NT, t % NH
                dve.wait_ge(work_full, n)
                dve.reduce_max(max2[:, h, tile, half:half + 1], ps, AX_X).then_inc(work_free, 1)

            def max_join():
                dve.wait_ge(work_free, work.upto())
                dve.tensor_tensor(max_cols[:, 0:2, 0:NT], max2[:, :, :, 0], max2[:, :, :, 1], ALU.max).then_inc(max_ready, 1)

            def max_rows(pairs):
                n, ps = work.next()
                dve.wait_ge(work_full, n)
                dve.wait_ge(scores_full, pairs * 2 * NT)
                for h in range(2):
                    of = ps[32 * h:32 * h + NT, 0:P].unsqueeze(1).to_broadcast([NT, NT, P])
                    to = q_b[D - h * D:D - h * D + NT, h].rearrange("p (j t) -> p j t", j=NT)
                    ins = dve.tensor_tensor(to, of, mask[32 * h:32 * h + NT, :, :], ALU.mult)
                ins.then_inc(work_free, 1)

            def v_tile(b, i):
                n, ps = work.next()
                dve.wait_ge(work_full, n)
                if i == 0:
                    dve.wait_ge(pv_done, ONE + b * PAIRS * NT)
                dve.tensor_copy(v_t[:, i], ps).then_inc(work_free, 1)

            def invert_sums(b, pair, h):
                if pair < PAIRS - 1:
                    n, ps = work.next()
                    dve.wait_ge(work_full, n)
                    read = work_free
                else:
                    ps, read = bank(h), end_sums_read
                    dve.wait_ge(end_sums_full, b * SUMS + h + 1)
                dve.wait_ge(o_normed, ONE + b * PAIRS * NH + pair * NH + h)
                dve.reciprocal(recip, ps).then_inc(read, 1)

            def normalise(b, pair, h, later=0):
                cols = slice(h * HALF, (h + 1) * HALF)
                if h == 0:
                    dve.wait_ge(o_ready, ONE + b * PAIRS + pair + 1)
                if pair < PAIRS - 1:
                    dve.wait_ge(work_free, work.upto(later))
                else:
                    dve.wait_ge(end_sums_read, ONE + b * SUMS + h + 1)
                dve.tensor_tensor(o32[:, cols], o32[:, cols], recip, ALU.mult).then_inc(o_normed, 1)

            def add_last(i, b, p):
                if i == 1:
                    dve.wait_ge(work_full, sums_used(b, p, True))
                dve.wait_ge(probs_ready, ONE + b * PAIRS * 2 * NT + p * 2 * NT + 2 * i + 2)
                if i > 1:
                    dve.wait_ge(last_sums, i - 1)
                dve.tensor_tensor(p_sum[:, 1], probs[:, 0, 1] if i == 1 else p_sum[:, 1], probs[:, i % 2, 1],
                                  ALU.add).then_inc(last_sums, 1)

            def hid_lo(b, pair, h):
                cols = slice(h * HALF, (h + 1) * HALF)
                dve.wait_ge(hid_hi_done, b * PAIRS * NH + pair * NH + h + 1)
                dve.scalar_tensor_tensor(out=hid[:, LO, pair, cols], in0=o32[:, cols],
                                         scalar=bqkv_c[:, 2 * CT + pair:2 * CT + pair + 1],
                                         in1=f(hid[:, HI, pair, cols]), op0=ALU.add, op1=ALU.subtract).then_inc(hid_lo_done, 1)

            dve.sem_inc(hid_lo_done, ONE)
            dve.sem_inc(o_normed, ONE)
            dve.sem_inc(end_sums_read, ONE)
            dve.wait_ge(pads_ready, 10)
            dve.wait_ge(norm_ready, 1)
            dve.wait_ge(y_first_loaded, 16)
            for u in range(NH * CT + 1):
                if u < NH * CT:
                    j, cols = u % CT, slice(u // CT * HALF, (u // CT + 1) * HALF)
                    dve.tensor_scalar(y_first[:, j, cols], y_first[:, j, cols], xn_scale[:, j, 0:1], xn_bias[:, j, 0:1],
                                      ALU.mult, ALU.add).then_inc(xn_made, 1)
                if u:
                    j, cols = (u - 1) % CT, slice((u - 1) // CT * HALF, ((u - 1) // CT + 1) * HALF)
                    dve.wait_ge(xn_hi_done, u)
                    dve.tensor_tensor(xn[:, LO, j, cols], y_first[:, j, cols], f(xn[:, HI, j, cols]), ALU.subtract).then_inc(xn_lo_done, 1)
            for i in range(QK):
                qk_lo(0, 0, i, 0)
            for t in range(SMAX):
                max_tile(t)
            max_join()
            max_rows(0)

            def batch1(b, last):
                work.start(b)
                for p in range(PAIRS):
                    more = p < PAIRS - 1 or not last
                    par, pairs = (p + 1) % 2, b * PAIRS + p

                    def next_qk(i):
                        if more:
                            qk_lo((p + 1) % PAIRS, par, i, (pairs + 1) * QK)

                    next_qk(0)
                    if p:
                        invert_sums(b, p - 1, 0)
                    next_qk(1)
                    if p:
                        normalise(b, p - 1, 0, 1 if more else 0)
                        invert_sums(b, p - 1, 1)
                        normalise(b, p - 1, 1)
                    if not more:
                        add_last(1, b, p)
                    next_qk(2)
                    if p:
                        hid_lo(b, p - 1, 0)
                    if p == 1 and not last:
                        dve.wait_ge(xn_hi_done, (b + 1) * NH * CT)
                        for i, of in enumerate((xn_scale, xn_bias)):
                            dve.tensor_copy(next_norm[:, i], of[:, :, bass.ds(b + 1, 1)].rearrange("p j a -> p (j a)")).then_inc(next_norm_ready, 1)
                    next_qk(3)
                    if not more:
                        hid_lo(b, p - 1, 1)
                        for i in range(2, NT):
                            add_last(i, b, p)
                    if more:
                        dve.wait_ge(max_ready, pairs + 1)
                        for t in range(SMAX):
                            if p and t == HID_ROW:
                                hid_lo(b, p - 1, 1)
                            if p == 2 and not last:
                                for u in range(NH * CT):
                                    if LO_ROW[u] == t:
                                        norm_lo(b + 1, u)
                            max_tile(t)
                        max_join()
                        max_rows(pairs + 1)
                for i in range(NT):
                    if not last:
                        v_tile(b + 1, i)
                    if i in (2, 4):
                        invert_sums(b, PAIRS - 1, i // 2 - 1)
                        normalise(b, PAIRS - 1, i // 2 - 1)
                    if i == (2 if last else 5):
                        hid_lo(b, PAIRS - 1, 0)
                    if i == 6:
                        hid_lo(b, PAIRS - 1, 1)
                for o, half in proj_tiles(last):
                    n, ps = work.next()
                    cols = slice(half * HALF, (half + 1) * HALF)
                    dve.wait_ge(work_full, n)
                    dve.wait_ge(res_scaled, b * CT + o + 1)
                    dve.tensor_tensor(res32[:, o, cols], ps, res32[:, o, cols], ALU.add).then_inc(work_free, 1)

            with dve.Fori(0, B - 1) as b:
                batch1(b, False)
            batch1(B - 1, True)

        @block.tensor
        def _(pe):
            def product(to, pairs):
                for i, (w, m) in enumerate(pairs):
                    last = pe.matmul(to, w, m, start=(i == 0), stop=(i == len(pairs) - 1))
                return last

            def transpose_x(b, n, first=False):
                if n % (NT // NH) == 0:
                    pe.wait_ge(x_loaded[n // (NT // NH)], b * 16 + 16)
                if n >= 4 or not first:
                    pe.wait_ge(lo_done, b * SPLITS + n - 3)
                for j in range(CT):
                    last = pe.transpose(ring_bank(n)[:, j * P:(j + 1) * P], x32[:, j, n * P:(n + 1) * P], eye)
                last.then_inc(ring_full, 1)

            def four_tiles(to, split0, before_tile, stationary, moving, done):
                def step(o, j):
                    for i, (w, m) in enumerate(THREE):
                        last = pe.matmul(to(o), stationary(w, j, o), moving(m, j), start=(j == 0 and i == 0),
                                         stop=(j == CT - 1 and i == 2))
                    return last

                for j in range(2):
                    pe.wait_ge(lo_done, split0 + j + 1)
                    for o in range(CT):
                        if j == 0 and before_tile:
                            before_tile(o)
                        step(o, j)
                pe.wait_ge(lo_done, split0 + CT)
                for o in range(CT):
                    step(o, 2)
                    step(o, 3).then_inc(done, 1)

            def batch(b, first, last_batch):
                def gram(n):
                    pe.wait_ge(lo_done, b * SPLITS + n + 1)
                    for g in range(CT):
                        if n == 0 and not first:
                            pe.wait_ge(y_ready, b * NH * CT - CT + g + 1)
                        for i, (w, m) in enumerate(THREE):
                            last = pe.matmul(bank(g)[:, G_FROM[g]:], xt[:, n % XT_SLOTS, w, g * P:(g + 1) * P],
                                             xt[:, n % XT_SLOTS, m, G_FROM[g]:],
                                             start=(n == 0 and i == 0), stop=(n == NT - 1 and i == 2))
                        if n == NT - 1:
                            last.then_inc(g_full, 1)
                        elif g == CT - 1:
                            last.then_inc(xt_used, 1)

                if first:
                    for n in range(AHEAD):
                        transpose_x(b, n, first)
                for n in range(NT):
                    if n + AHEAD < NT:
                        transpose_x(b, n + AHEAD, first)
                    gram(n)
                    if n == NT - 1:
                        pe.sem_inc(xt_used, 1)
                if first:
                    pe.wait_ge(w_lo_done, 1)
                def transpose_g(part, i):
                    to = mirror(part, i)[1]
                    for k in range(i + 1, CT):
                        last = pe.transpose(to[:, k - i - 1], f(gs[:, part, i, k * P:(k + 1) * P]), eye)
                    return last

                def t_product(o, j):
                    for i, (w, m) in enumerate(THREE):
                        last = pe.matmul(ring_bank(T0 + o), gs[:, w, j, o * P:(o + 1) * P], w_v[:, m, j],
                                         start=(j == 0 and i == 0), stop=(j == CT - 1 and i == 2))
                    return last

                pe.wait_ge(lo_done, b * SPLITS + G_S + 1)
                transpose_g(HI, 0).then_inc(mirror_full, 1)
                t_product(0, 0)
                t_product(1, 0)
                pe.wait_ge(lo_done, b * SPLITS + G_S + 2)
                transpose_g(LO, 0).then_inc(mirror_full, 1)
                t_product(2, 0)
                t_product(3, 0)
                pe.wait_ge(mirror_hi_done, 2 * b + 1)
                pe.wait_ge(mirror_lo_done, 2 * b + 1)
                t_product(0, 1)
                t_product(1, 1)
                transpose_g(HI, 1).then_inc(mirror_full, 1)
                transpose_g(LO, 1).then_inc(mirror_full, 1)
                t_product(2, 1)
                t_product(3, 1)
                pe.wait_ge(mirror_hi_done, 2 * b + 2)
                pe.wait_ge(mirror_lo_done, 2 * b + 2)
                pe.wait_ge(lo_done, b * SPLITS + G_S + 4)
                for o in range(CT):
                    t_product(o, 2)
                    t_product(o, 3).then_inc(ring_full, 1)
                pe.wait_ge(x_summed, (b + 1) * (CT + 2))
                product(bank(3)[0:2, :], [(s_s[:, j], w_v[:, m, j]) for j in range(CT) for m in (HI, LO)]).then_inc(row_full, 1)
                if first:
                    pe.wait_ge(w_lo_done, 2)
                for o in range(CT):
                    pe.wait_ge(lo_done, b * SPLITS + T_S + o + 1)
                    for g in range(CT):
                        window = slice(g // 2 * 2 * P, (g // 2 + 1) * 2 * P)
                        if o == 0 and g == 3:
                            pe.wait_ge(row_ready, 2 * b + 1)
                        for i, (t, w) in enumerate(THREE):
                            pe.matmul(bank(g)[:, 0:2 * P], ts[:, t, o, g * P:(g + 1) * P], w_q[:, w, o, window],
                                      start=(o == 0 and i == 0), stop=False)
                        if o == CT - 1:
                            pe.matmul(bank(g)[:, 0:2 * P], two_rows[0:2, g * P:(g + 1) * P], bias_rows[0:2, 0, window],
                                      start=False, stop=True).then_inc(m_full, 1)
                if first:
                    pe.wait_ge(w_lo_done, 4)
                for g in range(CT):
                    pe.wait_ge(m_split, b * 2 * CT + 2 * g + 2)
                    product(ring_bank(U0 + g), [(ms[:, i, g], w_o[:, k, g]) for i, k in THREE]).then_inc(ring_full, 1)
                for j in range(CT):
                    pe.wait_ge(lo_done, b * SPLITS + U_S + j + 1)
                    for m in (HI, LO):
                        last = pe.matmul(bank(3)[0:2, :], bk_s[:, j], us[:, m, j], start=(j == 0 and m == HI),
                                         stop=(j == CT - 1 and m == LO))
                last.then_inc(row_full, 1)
                four_tiles(lambda o: ring_bank(A0 + o), b * SPLITS + U_S, None,
                           lambda w, j, o: w_k[:, w, j, o * P:(o + 1) * P], lambda m, j: us[:, m, j], ring_full)
                pe.wait_ge(row_ready, 2 * b + 2)
                for o in range(CT):
                    last = pe.matmul(bank(3)[:, 2 * o:2 * o + 2], two_rows[0:2, o * P:(o + 1) * P], ones64[0:2, 0:2],
                                     start=True, stop=True)
                last.then_inc(c_full, 1)

                def wait_for_c(o):
                    if o == 3:
                        pe.wait_ge(c_ready, b + 1)

                four_tiles(bank, b * SPLITS + A_S, wait_for_c, lambda w, j, o: a_s[:, w, j, o * P:(o + 1) * P],
                           lambda m, j: xs[:, m, j, 0:HALF], y_full)
                if not last_batch:
                    for n in range(AHEAD):
                        transpose_x(b + 1, n)
                for o in range(CT):
                    pe.wait_ge(y_ready, b * NH * CT + o + 1)
                    product(bank(o), [(a_s[:, w, j, o * P:(o + 1) * P], xs[:, m, j, HALF:N])
                                      for j in range(CT) for w, m in THREE]).then_inc(y_full, 1)

            pe.wait_ge(consts_ready, 1)
            batch(0, True, False)
            with pe.Fori(1, B - 1) as b:
                batch(b, False, False)
            batch(B - 1, False, True)

            for i, of in enumerate((x1_mean, gn_in)):
                pe.wait_ge(gn_moved, i + 1)
                pe.matmul(bank(6 + i)[:, 0:CT * B], group_avg, of.rearrange("p j b -> p (j b)"),
                          start=True, stop=True).then_inc(gn_averaged, 1)
            work = Tally()

            def next_tile():
                n, ps = work.next()
                if work.started or work.n > 2:
                    pe.wait_ge(work_free, n - 2)
                return ps

            def qk_tile(slot, i, before=lambda j: None):
                piece, cols, to = i // 2, slice(i % 2 * HALF, (i % 2 + 1) * HALF), next_tile()
                for j in range(CT):
                    before(j)
                    for k, (w, m) in enumerate(THREE):
                        last = pe.matmul(to, w_s[:, slot, piece, w, j], xn[:, m, j, cols], start=(j == 0 and k == 0),
                                         stop=(j == CT - 1 and k == 2))
                last.then_inc(work_full, 1)

            def max_tile(par, t):
                h, tile, half = t // (NT * NH), t // NH % NT, t % NH
                pe.matmul(next_tile(), q_a[:, par, h, tile * P:(tile + 1) * P],
                          k_a[:, par, h, half * HALF:(half + 1) * HALF], start=True, stop=True).then_inc(work_full, 1)

            def max_turn(pairs):
                pe.wait_ge(max_ready, pairs + 1)
                pe.transpose(next_tile()[:, 0:P], max_cols.rearrange("p h t -> p (h t)"), eye).then_inc(work_full, 1)

            def v_tile(i):
                product(next_tile(), [(xn[:, m, j, i * P:(i + 1) * P], w_v1[:, :, w, j])
                                      for j in range(CT) for w, m in THREE]).then_inc(work_full, 1)

            def scores(pairs, par, i, between):
                for h in range(2):
                    pe.wait_ge(probs_ready, ONE + pairs * 2 * NT + 2 * max(i - 1, 0) + (h + 1 if i else 0))
                    keys = slice(i * P, (i + 1) * P)
                    for first, (k, q) in ((True, (k_a[:, par, h, keys], q_a[:, par, h])), (False, (k_b[:, par, h, keys], q_b[:, h]))):
                        for half in range(NH):
                            last = pe.matmul(psum[h][:, half], k, q[:, half * HALF:(half + 1) * HALF], start=first, stop=not first)
                            if not first and half == NH - 1:
                                last.then_inc(scores_full, 1)
                            between(4 * h + 2 * (not first) + half)

            def weigh(b, p, i, between):
                pairs = b * PAIRS + p
                pe.wait_ge(probs_ready, ONE + pairs * 2 * NT + 2 * i + 2)
                if i == 0:
                    pe.wait_ge(o_ready, ONE + pairs)
                for half in range(NH):
                    for h in range(2):
                        head = slice((2 * p + h) * D, (2 * p + h + 1) * D)
                        last = pe.matmul(psum[2][h * D:(h + 1) * D, half], v_t[:, i, head],
                                         probs[:, i % 2, h, half * HALF:(half + 1) * HALF], start=(i == 0), stop=(i == NT - 1))
                    if half == NH - 1:
                        last.then_inc(pv_done, 1)
                    between(8 + half)

            def sums(pairs, half, ps, done, last=False):
                if last:
                    pe.wait_ge(sum_step, LAST_SUMS + NT - 1)
                    pe.wait_ge(last_sums, NT - 1)
                else:
                    pe.wait_ge(sum_step, ONE + (pairs + 1) * 2 * (NT - 1))
                for h in range(2):
                    ins = pe.matmul(ps[h * D:(h + 1) * D, :], ones64, p_sum[:, h, half * HALF:(half + 1) * HALF],
                                     start=True, stop=True)
                ins.then_inc(done, 1)

            pe.sem_inc(pv_done, ONE)
            pe.wait_ge(ws_loaded[1], 16)
            for i in range(QK):
                if i < NH:
                    qk_tile(1, i, lambda j: pe.wait_ge(xn_lo_done, i * CT + j + 1))
                else:
                    qk_tile(1, i)
            pe.wait_ge(wv1_loaded, 16)
            rows_made = 0
            for i in range(NT):
                if i >= CT:
                    pe.wait_ge(v_first_done, i - CT + 1)
                for j in range(CT):
                    for k, (w, m) in enumerate(THREE):
                        last = pe.matmul(bank(i % CT), xn[:, m, j, i * P:(i + 1) * P], w_v1[:, :, w, j],
                                         start=(j == 0 and k == 0), stop=(j == CT - 1 and k == 2))
                    if j == CT - 1:
                        last.then_inc(v_first_full, 1)
                    if i:
                        max_tile(0, rows_made)
                        rows_made += 1
                if i < SMAX - (NT - 1) * CT:
                    if i == 0:
                        pe.wait_ge(k_twice, QK)
                        pe.wait_ge(work_free, QK)
                    max_tile(0, rows_made)
                    rows_made += 1
            assert rows_made == SMAX
            max_turn(0)
            pe.wait_ge(v_first_done, NT)

            def batch1(b, last):
                work.start(b)
                loads = b * ((PAIRS + 2) // 2)
                for p in range(PAIRS):
                    more = p < PAIRS - 1 or not last
                    par, pairs = p % 2, b * PAIRS + p
                    def next_qk(i):
                        if more:
                            if i == 0:
                                slot = p % 2
                                pe.wait_ge(ws_loaded[slot], (loads + p // 2 + 1 + slot) * 16)
                                if p == PAIRS - 1:
                                    pe.wait_ge(xn_lo_done, (b + 2) * NH * CT)
                            qk_tile(p % 2, i)

                    next_qk(0)
                    for i in range(NT):
                        def next_row(place):
                            for t, at in enumerate(ROW_PLACES[i]):
                                if more and at == place:
                                    if i == 2 and t == 0:
                                        pe.wait_ge(work_free, work.upto())
                                        pe.wait_ge(k_twice, (pairs + 2) * QK)
                                    max_tile(1 - par, sum(ROWS[:i]) + t)

                        if i == 0 and p == 0:
                            pe.wait_ge(end_sums_read, ONE + b * SUMS)
                        if i == 0:
                            pe.wait_ge(q_b_ready, 2 * pairs + 2)
                            pe.wait_ge(work_free, work.upto(1 if more else 0))
                        scores(pairs, par, i, next_row)
                        if p and i < NH:
                            sums(pairs - 1, i, next_tile(), work_full)
                        if i == 0:
                            next_qk(1)
                        if i == 1:
                            next_qk(2)
                        if i:
                            weigh(b, p, i - 1, next_row)
                        if i == 1:
                            next_qk(3)

                    def turn(place):
                        if more and place == 8:
                            max_turn(pairs + 1)

                    weigh(b, p, NT - 1, turn)
                for i in range(NT):
                    if not last:
                        v_tile(i)
                    if i in (2, 4):
                        sums(b * PAIRS + PAIRS - 1, i // 2 - 1, bank(i // 2 - 1), end_sums_full, last)
                for t, (o, half) in enumerate(proj_tiles(last)):
                    cols = slice(half * HALF, (half + 1) * HALF)
                    slot, piece = o // 2, o % 2
                    if o == 0:
                        pe.wait_ge(hid_lo_done, ONE + (b + 1) * PAIRS * NH - (NH - 1 - half))
                    if half == 0 and piece == 0:
                        n_load = (loads + 3 + slot) - (1 if last and slot else 0)
                        pe.wait_ge(ws_loaded[slot], n_load * 16)
                    product(next_tile(), [(w_s[:, slot, piece, w, j], hid[:, m, j, cols])
                                          for j in range(CT) for w, m in THREE]).then_inc(work_full, 1)

            with pe.Fori(0, B - 1) as b:
                batch1(b, False)
            batch1(B - 1, True)



def kernel(**inputs):
    import numpy as _np
    import concourse.bacc as _bacc
    from concourse import mybir as _mybir
    from concourse.bass_utils import run_bass_kernel_spmd as _run

    a = {k: _np.asarray(v) for k, v in inputs.items()}
    qkv, proj = a["L1_conv_w_qkv"], a["L1_conv_w_proj"]
    order = [qkv[i * C + p * P:i * C + (p + 1) * P] for p in range(CT) for i in range(2)]
    order += [proj[p * P:(p + 1) * P] for p in range(CT)]
    order += [qkv[2 * C + p * P:2 * C + (p + 1) * P] for p in range(CT)]
    w1 = _np.stack([w.T.reshape(CT, P, P).transpose(1, 0, 2) for w in order])
    host = {
        "x": a["x"].reshape(B, C, N),
        "wq_t": a["L0_conv_Wq"].T, "wv_t": a["L0_conv_Wv"].T, "wk": a["L0_conv_Wk"], "wo_t": a["L0_conv_Wo"].T,
        "bq0": a["L0_conv_bq"], "bv0": a["L0_conv_bv"], "bk0": a["L0_conv_bk"], "bo0": a["L0_conv_bo"],
        "gamma0": a["L0_conv_gamma"], "beta0": a["L0_conv_beta"],
        "gamma1": a["L1_conv_gamma"], "beta1": a["L1_conv_beta"],
        "w1": w1, "bqkv1": a["L1_conv_b_qkv"], "bproj1": a["L1_conv_b_proj"],
    }
    nc = _bacc.Bacc("TRN2", target_bir_lowering=False, num_devices=1)
    arrays, args = {}, []
    for name, v in host.items():
        v = _np.ascontiguousarray(v)
        arrays[name] = v
        args.append(nc.dram_tensor(name, v.shape, _mybir.dt.from_np(v.dtype), kind="ExternalInput").ap())
    args.append(nc.dram_tensor("out", (B, C, N), F32, kind="ExternalOutput").ap())
    build(nc, *args)
    r = _run(nc, [arrays], core_ids=[0])
    return r.results[0]["out"].reshape(B, C, 32, 32)
```
